# Optimizing a Trainium2 kernel written in Bass

```python
import numpy as np
import jax
import jax.numpy as jnp

def _softmax(x, axis=-1):
    return jax.nn.softmax(x, axis=axis)

def _gelu(x):
    return jax.nn.gelu(x, approximate=True)

def _silu(x):
    return jax.nn.silu(x)

def _sigmoid(x):
    return jax.nn.sigmoid(x)

def _layernorm(x, axis=-1, eps=1e-05):
    m = jnp.mean(x, axis=axis, keepdims=True)
    v = jnp.var(x, axis=axis, keepdims=True)
    return (x - m) / jnp.sqrt(v + eps)

def _scatter_add(tgt, idx, src, axis=0):
    return tgt.at[idx].add(src)

def _segment_sum(src, seg, n):
    return jax.ops.segment_sum(src, seg, n)
kernel_name = 'mk_audio_tower_d1_tok_audfeat512_r4_e307fc'

def setup_inputs(seed: int=0):
    np.random.seed(seed)
    _w = jnp.asarray

    def _rec_inputs():
        import jax
        import jax.numpy as jnp
        _rk = jax.random.key(seed)
        x = -0.000125008 + 0.999885 * jax.random.normal(jax.random.fold_in(_rk, 1), (128, 256, 128), jnp.float32)
        return x
    x = _rec_inputs()

    def _L0_tok_setup():
        import jax, jax.numpy as jnp
        import numpy as np
        TOKEN_DIM = 4
        EPS = 1e-06
        key = jax.random.key(seed)
        k_x, k_w = jax.random.split(key)
        B, S, E = (8, 2048, 128)
        EMB = 128
        x = jax.random.normal(k_x, (B, S, E), dtype=jnp.float32)
        ln_gamma = jnp.ones((E,), dtype=jnp.float32)
        ln_beta = jnp.zeros((E,), dtype=jnp.float32)
        W = jax.random.normal(k_w, (TOKEN_DIM * E, EMB), dtype=jnp.float32) * 0.02
        b = jnp.zeros((EMB,), dtype=jnp.float32)
        return {'x': x, 'ln_gamma': ln_gamma, 'ln_beta': ln_beta, 'W': W, 'b': b}
    _L0_tok_all = _L0_tok_setup()
    _L0_tok_in = {k: v for k, v in _L0_tok_all.items() if k in ('ln_gamma', 'ln_beta', 'W', 'b')}
    del _L0_tok_all

    def _L0_attn_setup():
        import jax, jax.numpy as jnp
        import numpy as np
        import math
        B, L, DIM, H = (2, 512, 128, 8)
        key = jax.random.key(seed)
        ks = jax.random.split(key, 8)
        s = 0.02
        return {'x': jax.random.normal(ks[0], (B, L, DIM), dtype=jnp.float32), 'Wq': jax.random.normal(ks[1], (DIM, DIM), dtype=jnp.float32) * s, 'Wk': jax.random.normal(ks[2], (DIM, DIM), dtype=jnp.float32) * s, 'Wv': jax.random.normal(ks[3], (DIM, DIM), dtype=jnp.float32) * s, 'Wb': jax.random.normal(ks[4], (H, DIM), dtype=jnp.float32) * s, 'mixing': jax.random.normal(ks[5], (H, DIM), dtype=jnp.float32) * 0.2, 'Wd': jax.random.normal(ks[6], (DIM, DIM), dtype=jnp.float32) * s, 'bd': jax.random.normal(ks[7], (DIM,), dtype=jnp.float32) * s}
    _L0_attn_all = _L0_attn_setup()
    _L0_attn_in = {k: v for k, v in _L0_attn_all.items() if k in ('Wq', 'Wk', 'Wv', 'Wb', 'mixing', 'Wd', 'bd')}
    del _L0_attn_all

    def _L0_ffn_setup():
        import jax, jax.numpy as jnp
        import numpy as np
        EPS = 1e-09
        LN_EPS = 1e-05

        def _layernorm(x, gamma):
            x = x.astype(jnp.float32)
            mu = jnp.mean(x, axis=-1, keepdims=True)
            var = jnp.var(x, axis=-1, keepdims=True)
            return (x - mu) * jax.lax.rsqrt(var + LN_EPS) * gamma
        key = jax.random.key(seed)
        ks = jax.random.split(key, 5)
        b, n, d, e, h = (4, 256, 128, 6, 512)
        x = jax.random.normal(ks[0], (b, n, d), dtype=jnp.float32)
        w_gating = jax.random.normal(ks[1], (d, e), dtype=jnp.float32)
        std1 = 1.0 / np.sqrt(h)
        std2 = 1.0 / np.sqrt(d)
        w1 = jax.random.uniform(ks[2], (e, d, h), jnp.float32, -std1, std1)
        w2 = jax.random.uniform(ks[3], (e, h, d), jnp.float32, -std2, std2)
        gamma = jnp.ones((d,), dtype=jnp.float32)
        return {'x': x, 'w_gating': w_gating, 'gamma': gamma, 'w1': w1, 'w2': w2}
    _L0_ffn_all = _L0_ffn_setup()
    _L0_ffn_in = {k: v for k, v in _L0_ffn_all.items() if k in ('w_gating', 'gamma', 'w1', 'w2')}
    del _L0_ffn_all
    return {'x': x, 'L0_tok_ln_gamma': _L0_tok_in['ln_gamma'], 'L0_tok_ln_beta': _L0_tok_in['ln_beta'], 'L0_tok_W': _L0_tok_in['W'], 'L0_tok_b': _L0_tok_in['b'], 'L0_attn_Wq': _L0_attn_in['Wq'], 'L0_attn_Wk': _L0_attn_in['Wk'], 'L0_attn_Wv': _L0_attn_in['Wv'], 'L0_attn_Wb': _L0_attn_in['Wb'], 'L0_attn_mixing': _L0_attn_in['mixing'], 'L0_attn_Wd': _L0_attn_in['Wd'], 'L0_attn_bd': _L0_attn_in['bd'], 'L0_ffn_w_gating': _L0_ffn_in['w_gating'], 'L0_ffn_gamma': _L0_ffn_in['gamma'], 'L0_ffn_w1': _L0_ffn_in['w1'], 'L0_ffn_w2': _L0_ffn_in['w2']}

def reference(x, L0_tok_ln_gamma, L0_tok_ln_beta, L0_tok_W, L0_tok_b, L0_attn_Wq, L0_attn_Wk, L0_attn_Wv, L0_attn_Wb, L0_attn_mixing, L0_attn_Wd, L0_attn_bd, L0_ffn_w_gating, L0_ffn_gamma, L0_ffn_w1, L0_ffn_w2):
    import jax
    import jax.numpy as jnp

    def _L0_tok_ref(x, ln_gamma, ln_beta, W, b):
        import jax, jax.numpy as jnp
        import numpy as np
        TOKEN_DIM = 4
        EPS = 1e-06
        B, S, E = x.shape
        mean = jnp.mean(x, axis=-1, keepdims=True)
        var = jnp.mean(jnp.square(x - mean), axis=-1, keepdims=True)
        h = (x - mean) * jax.lax.rsqrt(var + EPS) * ln_gamma + ln_beta
        h = h.reshape(B, S // TOKEN_DIM, TOKEN_DIM * E)
        out = jnp.einsum('bsf,fd->bsd', h, W) + b
        return jax.nn.gelu(out, approximate=False)

    def _L0_attn_ref(x, Wq, Wk, Wv, Wb, mixing, Wd, bd):
        import jax, jax.numpy as jnp
        import numpy as np
        import math
        B, L, DIM, H = (2, 512, 128, 8)
        b, l, d = x.shape
        h = mixing.shape[0]
        dh = d // h
        q = x @ Wq.T
        k = x @ Wk.T
        v = (x @ Wv.T).reshape(b, l, h, dh).transpose(0, 2, 1, 3)
        scores = jnp.einsum('bld,hd,bsd->bhls', q, mixing, k)
        cb = jnp.einsum('bsd,hd->bhs', x, Wb)
        scale = math.sqrt(d / h)
        scores = (scores + cb[:, :, None, :]) / scale
        probs = jax.nn.softmax(scores, axis=-1)
        ctx = jnp.einsum('bhls,bhsd->bhld', probs, v)
        ctx = ctx.transpose(0, 2, 1, 3).reshape(b, l, d)
        return ctx @ Wd.T + bd

    def _L0_ffn_ref(x, w_gating, gamma, w1, w2):
        import jax, jax.numpy as jnp
        import numpy as np
        EPS = 1e-09
        LN_EPS = 1e-05

        def _layernorm(x, gamma):
            x = x.astype(jnp.float32)
            mu = jnp.mean(x, axis=-1, keepdims=True)
            var = jnp.var(x, axis=-1, keepdims=True)
            return (x - mu) * jax.lax.rsqrt(var + LN_EPS) * gamma
        b, n, d = x.shape
        E = w_gating.shape[-1]
        C = max(min(n, int(n * 6.0 / E)), 4)
        raw = jnp.einsum('bnd,de->bne', x, w_gating)
        probs = jax.nn.softmax(raw, axis=-1)
        gate1 = jnp.max(probs, axis=-1)
        idx1 = jnp.argmax(probs, axis=-1)
        mask1 = jax.nn.one_hot(idx1, E, dtype=jnp.float32)
        gates_wo1 = probs * (1.0 - mask1)
        gate2 = jnp.max(gates_wo1, axis=-1)
        denom = gate1 + gate2 + EPS
        gate1 = gate1 / denom
        pos1 = (jnp.cumsum(mask1, axis=-2) - mask1) * mask1
        mask1 = mask1 * (pos1 < float(C)).astype(jnp.float32)
        mask1_flat = jnp.sum(mask1, axis=-1)
        pos1_flat = jnp.sum(pos1, axis=-1).astype(jnp.int32)
        gate1 = gate1 * mask1_flat
        combine = gate1[..., None, None] * mask1_flat[..., None, None] * jax.nn.one_hot(idx1, E, dtype=jnp.float32)[..., None] * jax.nn.one_hot(pos1_flat, C, dtype=jnp.float32)[..., None, :]
        dispatch = (combine != 0).astype(jnp.float32)
        expert_in = jnp.einsum('bnd,bnec->ebcd', x, dispatch)
        xn = _layernorm(expert_in, gamma)
        hidden = jax.nn.gelu(jnp.einsum('ebcd,edh->ebch', xn, w1), approximate=False)
        expert_out = jnp.einsum('ebch,ehd->ebcd', hidden, w2)
        out = jnp.einsum('ebcd,bnec->bnd', expert_out, combine)
        return out
    h = _L0_tok_ref(x, L0_tok_ln_gamma, L0_tok_ln_beta, L0_tok_W, L0_tok_b)
    h = h + _L0_attn_ref(_layernorm(h, axis=-1), L0_attn_Wq, L0_attn_Wk, L0_attn_Wv, L0_attn_Wb, L0_attn_mixing, L0_attn_Wd, L0_attn_bd)
    h = h + _L0_ffn_ref(_layernorm(h, axis=-1), L0_ffn_w_gating, L0_ffn_gamma, L0_ffn_w1, L0_ffn_w2)
    return h

_drawn_inputs = setup_inputs


def setup_inputs(seed=0):
    import zlib

    import numpy as np

    out = dict(_drawn_inputs(seed))
    spreads = {'L0_tok_ln_gamma': (1.0, 0.2),
     'L0_tok_ln_beta': (0.0, 0.1),
     'L0_tok_b': (0.0, 0.1),
     'L0_ffn_gamma': (1.0, 0.2)}
    factors = {'L0_attn_Wq': 7.374, 'L0_attn_Wk': 6.551, 'L0_attn_Wb': 3.961, 'L0_attn_mixing': 6.506}
    for name, (base, spread) in spreads.items():
        noise = np.random.default_rng([zlib.crc32(name.encode()), seed]).standard_normal(out[name].shape)
        drawn = base * np.exp(spread * noise) if base else spread * noise
        out[name] = jnp.asarray(drawn.astype(out[name].dtype))
    for name, factor in factors.items():
        out[name] = (out[name] * factor).astype(out[name].dtype)
    return out
```

```python
from contextlib import ExitStack

import numpy as np

import concourse.bass as bass
from concourse import mybir

F32 = mybir.dt.float32
BF16 = mybir.dt.bfloat16
I32 = mybir.dt.int32
ALU = mybir.AluOpType
ACT = mybir.ActivationFunctionType
X = mybir.AxisListType.X

P = 128
D = 128
TOK = 4
SEQ = 64
H = 8
DH = D // H
HP = H // 2
VW = DH + 1
E = 6
HID = 512
HC = HID // P
N = 8192
NT = N // P
T = 4
NG = NT // T
REGION = N + P
NX = E - 1 + -(-(N - (E - 1)) // P)
SPARE = NX - NT + 1
ROWW = 132
GATE, TOKEN, SCALE, SHIFT = 128, 129, 130, 131
EPS_TOK, EPS = 1e-6, 1e-5

C_ID, C_TRI, C_ONE, C_IND, C_SEL, C_IOTA, C_BASE, C_HALF, C_TILE = 0, 128, 256, 384, 512, 640, 664, 672, 688
C_END = C_TILE + NX * E


def constants():
    c = np.zeros((P, C_END), np.float32)
    p = np.arange(P)
    c[:, C_ID:C_ID + P] = np.eye(P)
    c[:, C_TRI:C_TRI + P] = p[:, None] < p[None, :]
    c[:, C_ONE:C_ONE + P] = 1.0
    for r in range(6):
        c[r, C_IND + SEQ * (r % 2):C_IND + SEQ * (r % 2) + SEQ] = 1.0
    c[0:96:32, C_SEL:C_SEL + P] = 1.0
    c[:, C_IOTA:C_IOTA + T * E] = np.tile(np.arange(E) - 8.0, T)
    c[:, C_BASE:C_BASE + E] = np.arange(E) * REGION
    c[:, C_HALF:C_HALF + 16] = -0.5
    c[:, C_TILE:C_END] = np.repeat(np.arange(NX), E)
    i = np.zeros((P, NT + 1), np.int32)
    i[:, 0:NT] = p[:, None] + P * np.arange(NT)[None, :]
    i[:, NT] = N + p
    return c, i


def need(eng, sem, value):
    if not isinstance(value, int) or value > 0:
        eng.wait_ge(sem, value)


def build(nc, x, w_tok, g_tok, b_tok, bias_tok, wq_t, wk_t, wv_t, wb_t, mix_t, wd_t, bd, w_gate, g_ffn, w1, w2,
          cf, ci, rows, out):
    ctx = ExitStack()
    with ctx:
        def sb(name, shape, dt=F32):
            return ctx.enter_context(nc.sbuf_tensor(name, shape, dt))

        def sem(name):
            return ctx.enter_context(nc.semaphore(name))

        bank = [ctx.enter_context(nc.psum_tensor(f"bank{i}", [P, 512], F32)) for i in range(8)]

        cst = sb("cst", [P, C_END])
        cint = sb("cint", [P, NT + 1], I32)
        ident = cst[:, C_ID:C_ID + P]
        neg_half = cst[:, C_HALF:C_HALF + 16]
        ident_bf = sb("ident_bf", [P, P], BF16)
        tri_bf = sb("tri_bf", [P, P], BF16)
        ones_bf = sb("ones_bf", [P, P], BF16)
        ind_bf = sb("ind_bf", [P, P], BF16)
        sel_bf = sb("sel_bf", [P, P], BF16)
        w_raw = sb("w_raw", [P, TOK, D])
        w_sc = sb("w_sc", [P, TOK, D])
        cols = sb("cols", [P, 4])
        beta_bc = sb("beta_bc", [P, P])
        bias_row = sb("bias_row", [1, 2, D])
        bias_f = sb("bias_f", [P, 2, D])
        bias_hi = sb("bias_hi", [P, 2, D], BF16)
        bias_r = sb("bias_r", [P, 2, D])
        bias_mid = sb("bias_mid", [P, 2, D], BF16)
        bias_lo = sb("bias_lo", [P, 2, D], BF16)
        bias3 = sb("bias3", [P, 2, D], BF16)
        wqkvd = sb("wqkvd", [P, 4, D])
        wb_sb = sb("wb_sb", [P, H])
        mix_sb = sb("mix_sb", [P, H])
        wg_sb = sb("wg_sb", [P, E])
        w1_sb = sb("w1_sb", [P, E, HID])
        w2_sb = sb("w2_sb", [P, E, HC, D])
        tok_out = sb("tok_out", [P, NT, D])
        xs = sb("xs", [P, 2 * T, TOK, D])
        st1 = sb("st1", [P, 2, T * TOK, 6])
        sm1 = sb("sm1", [P, 10, T * TOK])
        rs1 = sb("rs1", [P, 2, T * TOK])
        nm1 = sb("nm1", [P, 2, T * TOK])
        xt = sb("xt", [P, 2, TOK * P])
        st2 = sb("st2", [P, 2, T, 6])
        sm2 = sb("sm2", [P, 10, T])
        rs2 = sb("rs2", [P, 2, T])
        nm2 = sb("nm2", [P, 2, T])
        xn = sb("xn", [P, 2, T, D])
        xnt = sb("xnt", [P, 2, T * P])
        qt = sb("qt", [P, 2, T * P])
        kt = sb("kt", [P, 2, T * P])
        kmix = sb("kmix", [P, 2, H, T * P])
        vb = sb("vb", [P, 2, 2 * T, HP, 2 * VW])
        cbf = sb("cbf", [P, T * H])
        cbr = sb("cbr", [P, T * H])
        cb3 = sb("cb3", [P, 3, T * H], BF16)
        cbt = sb("cbt", [96, P], BF16)
        cbrow = sb("cbrow", [P, 2, T * H, SEQ], BF16)
        mx = sb("mx", [P, 2, H])
        pr = sb("pr", [P, 2, H, SEQ])
        pe_ = sb("pe_", [P, 2, H * SEQ])
        pt = sb("pt", [P, 2, HP, P])
        rden = sb("rden", [P, 2, HP, 2])
        ctxn = sb("ctxn", [P, 2, T, D])
        ctxt = sb("ctxt", [P, T * P])
        st3 = sb("st3", [P, 2, T, 6])
        sm3 = sb("sm3", [P, 16, T])
        row = sb("row", [P, 4, T, ROWW])
        xg = sb("xg", [P, 2, T, D])
        xgt = sb("xgt", [P, T * P])
        rt = sb("rt", [P, 12, T, E])
        r4 = sb("r4", [P, 12, T])
        oh = sb("oh", [P, 5, E])
        oh_bf = sb("oh_bf", [P, T, E], BF16)
        base = sb("base", [P, E])
        pos = sb("pos", [P, 4, T], I32)
        te = sb("te", [1, 16, E])
        tei = sb("tei", [1, 2, E], I32)
        x_flat = xs[:, :, :, :].rearrange("p a j e -> p (a j e)")
        tg = x_flat[0:1, 0:2 * NX * E].rearrange("p (a i e) -> p a i e", a=2, e=E)
        tn = sb("tn", [1, 4, NX])
        ti = sb("ti", [1, 2, NX], I32)
        pad = sb("pad", [P, ROWW])
        er = sb("er", [P, 4, ROWW])
        ex = sb("ex", [P, 2, D])
        ext = sb("ext", [P, 2, P])
        hid = x_flat[:, 2048:2048 + 2 * HID].rearrange("p (k h) -> p k h", k=2)
        hidt = x_flat[:, 3072:3072 + 2 * HID].rearrange("p (k c t) -> p k c t", k=2, c=HC)
        eo = sb("eo", [P, 2, D])

        s_cst = sem("s_cst"); s_wtok = sem("s_wtok"); s_watt = sem("s_watt"); s_wexp = sem("s_wexp")
        s_set = sem("s_set")
        s_bias_ps = sem("s_bias_ps")
        x_in = [sem(f"x_in{i}") for i in range(2 * T)]
        a_stats = sem("a_stats"); a_small = sem("a_small"); a_coef = sem("a_coef")
        a_nv = sem("a_nv"); a_np = sem("a_np"); a_na = sem("a_na")
        a_tr = sem("a_tr"); a_ev = sem("a_ev"); a_mm = sem("a_mm"); a_out = sem("a_out")
        b_stats = sem("b_stats"); b_small = sem("b_small"); b_xn = sem("b_xn"); b_xtr = sem("b_xtr")
        b_xt = sem("b_xt"); b_cb = sem("b_cb"); b_cbf = sem("b_cbf"); b_cbs = sem("b_cbs"); b_cbtr = sem("b_cbtr")
        b_cbt = sem("b_cbt"); b_cbrow = [sem(f"b_cbrow{i}") for i in range(2)]
        b_q = sem("b_q"); b_qt = sem("b_qt"); b_k = sem("b_k"); b_kt = sem("b_kt")
        b_kmv = sem("b_kmv"); b_kma = sem("b_kma"); b_v = sem("b_v"); b_va = sem("b_va"); b_vv = sem("b_vv")
        b_sc = sem("b_sc"); b_mx = sem("b_mx"); b_sub = sem("b_sub"); b_exp = sem("b_exp"); b_ptr = sem("b_ptr")
        b_pt = sem("b_pt"); b_pv = sem("b_pv"); b_rd = sem("b_rd"); b_cn = sem("b_cn")
        c_tr = sem("c_tr"); c_ct = sem("c_ct"); c_wd = sem("c_wd"); c_res = sem("c_res"); c_stats = sem("c_stats")
        c_small = sem("c_small"); c_xg = sem("c_xg"); c_xtr = sem("c_xtr"); c_xt = sem("c_xt")
        c_gate = sem("c_gate"); c_rt = sem("c_rt"); c_exp = sem("c_exp"); c_pre = sem("c_pre")
        c_scat = [sem(f"c_scat{i}") for i in range(4)]
        s_tab = sem("s_tab"); s_pad = sem("s_pad"); s_padr = sem("s_padr"); s_w1s = sem("s_w1s")
        e_in = [sem(f"e_in{i}") for i in range(4)]
        e_n = sem("e_n"); e_tr = sem("e_tr"); e_xt = sem("e_xt"); e_f1 = sem("e_f1"); e_hid = sem("e_hid")
        e_htr = sem("e_htr"); e_ht = sem("e_ht"); e_f2 = sem("e_f2"); e_o = sem("e_o")
        e_out = [sem(f"e_out{i}") for i in range(2)]

        x_t = x.rearrange("a (s j) e -> (a s) (j e)", j=TOK)
        block = ctx.enter_context(nc.Block())

        def tile(n):
            return tok_out[:, bass.ds(n, 1), :].rearrange("p o d -> p (o d)")

        SMALL1 = 10
        SMALL2 = 12
        SMALL3 = 18
        ROUTE = 22
        S1, S2, S3, S4, S5, S6 = 1, 2, 3, 4, 5, 6

        def groups(eng, body, lag, first, ways):
            def runs_at(u):
                return lambda k: 0 <= u - k < NG
            for u in range(first):
                body(u, u % ways, runs_at(u))
            turns = (NG - first) // ways
            with eng.Fori(0, turns) as turn:
                for c in range(ways):
                    body(turn * ways + (first + c), (first + c) % ways, lambda k: True)
            for u in range(first + ways * turns, NG + lag):
                body(u, u % ways, runs_at(u))

        def stored(i, k):
            return 16 * (i // 2 + 1) if isinstance(i, int) else (i - k) * 8 + 16

        class Step:
            def __init__(self, i, c):
                self.i, self.c = i, c

            def __call__(self, s):
                return not isinstance(self.i, int) or 0 <= self.i - s < NX

            def k(self, s):
                return (self.c - s) % 2

            def slot(self, s):
                return (self.c - s) % 4

        def tiles3(eng, body, lag):
            for i in range(8):
                body(i, Step(i, i % 4))
            whole = (NX - 8) // 4
            with eng.Fori(0, whole) as four:
                for c in range(4):
                    body(four * 4 + (8 + c), Step(four, c))
            for i in range(8 + 4 * whole, NX + lag):
                body(i, Step(i, i % 4))

        @block.sync
        def _(sp):
            sp.dma_start(cst[:, :], cf).then_inc(s_cst, 16)
            sp.dma_start(cint[:, :], ci).then_inc(s_cst, 16)

            def load_x(i, slot, first):
                if not first:
                    sp.wait_ge(a_tr, i * 2 * T + slot - 2 * T + 1)
                sp.dma_start(xs[:, slot, :, :].rearrange("p j e -> p (j e)"),
                             x_t[bass.ds((i * 2 * T + slot) * P, P), :]).then_inc(x_in[slot], 16)

            for slot in range(2 * T):
                load_x(0, slot, True)
            with sp.Fori(1, NT // (2 * T)) as i:
                for slot in range(2 * T):
                    load_x(i, slot, False)
            for e in range(E):
                sp.dma_start(w1_sb[:, e, :], w1[e]).then_inc(s_wexp, 16)
                sp.dma_start(w2_sb[:, e, :, :], w2[e].rearrange("(c p) d -> p c d", p=P)).then_inc(s_wexp, 16)

            def body(u, par, runs):
                if runs(S1):
                    g = u - S1
                    k = (par - S1) % 2
                    need(sp, b_cbt, g + 1)
                    need(sp, b_sc, T * (g - 2) + T)
                    for r in range(6):
                        c, s = r // 2, r % 2
                        sp.dma_start(cbrow[r:r + 1, k, :, :],
                                     cbt[32 * c:32 * c + 32, SEQ * s:SEQ * s + SEQ].rearrange("a (o s) -> a o s", o=1)
                                     ).then_inc(b_cbrow[k], 16)
            groups(sp, body, S6, 8, 4)

            sp.wait_ge(s_padr, 4)
            for i in range(SPARE):
                sp.dma_start(rows[E * REGION + i * P:E * REGION + (i + 1) * P, :], pad[:, :]).then_inc(s_pad, 16)
            sp.wait_ge(s_tab, 20)
            for e in range(E):
                r = sp.value_load(tei[0:1, 0, e:e + 1], min_val=0, max_val=E * REGION - P)
                sp.dma_start(rows[bass.ds(r, P), :], pad[:, :]).then_inc(s_pad, 16)
            sp.wait_ge(s_pad, 16 * (SPARE + E))
            for k in range(4):
                sp.wait_ge(c_scat[k], 16 * T * NG // 4)

            def load_rows(i, slot):
                r = sp.value_load(ti[0:1, 0, bass.ds(i, 1)], min_val=0, max_val=E * REGION + SPARE * P - P)
                need(sp, e_o, i - 3)
                if not (isinstance(i, int) and i < 4):
                    need(sp, e_out[slot % 2], stored(i - 4, slot % 2))
                sp.dma_start(er[:, slot, :], rows[bass.ds(r, P), :]).then_inc(e_in[slot], 16)

            for i in range(4):
                load_rows(i, i)
            with sp.Fori(0, NX // 4 - 1) as four:
                for c in range(4):
                    load_rows(four * 4 + (4 + c), c)
            for i in range(NX - (NX % 4), NX):
                load_rows(i, i % 4)

        @block.gpsimd
        def _(pool):
            def after(sem_, value):
                if not isinstance(value, int):
                    pool.wait_ge(sem_, value)
                    pool.nop(nofuse=True)
                elif value > 0:
                    pool.wait_ge(sem_, value)

            after(s_cst, 32)
            nc.gpsimd.memset(pad[:, :], 0.0).then_inc(s_padr, 1)
            after(s_padr, 1)
            nc.gpsimd.tensor_copy(pad[:, TOKEN:TOKEN + 1].bitcast(I32), cint[:, NT:NT + 1]).then_inc(s_padr, 1)
            nc.gpsimd.memset(cbrow[:, 0, :, :], 0.0).then_inc(s_padr, 1)
            nc.gpsimd.memset(cbrow[:, 1, :, :], 0.0).then_inc(s_padr, 1)

            def variance(st, sm, n, sem_, v0):
                me, m2e, mo, m2o = (st[:, :, i] for i in (1, 2, 4, 5))
                pool_ = nc.gpsimd
                pool_.tensor_tensor(sm[:, 0, :], me, mo, ALU.subtract).then_inc(sem_, 1)
                pool_.tensor_tensor(sm[:, 1, :], m2e, m2o, ALU.add).then_inc(sem_, 1)
                pool_.tensor_tensor(sm[:, 4, :], me, mo, ALU.add).then_inc(sem_, 1)
                after(sem_, v0 + 3)
                pool_.tensor_tensor(sm[:, 2, :], sm[:, 0, :], sm[:, 0, :], ALU.mult).then_inc(sem_, 1)
                pool_.tensor_scalar(sm[:, 3, :], sm[:, 1, :], 1.0 / D, 0.0, ALU.mult, ALU.add).then_inc(sem_, 1)
                after(sem_, v0 + 5)
                pool_.tensor_scalar(sm[:, 5, :], sm[:, 2, :], 0.25, 0.0, ALU.mult, ALU.add).then_inc(sem_, 1)
                after(sem_, v0 + 6)
                pool_.tensor_tensor(sm[:, 6, :], sm[:, 5, :], sm[:, 3, :], ALU.add).then_inc(sem_, 1)
                after(sem_, v0 + 7)

            def rstd(st, sm, n, eps, rs, nm, sem_, v0):
                pool_ = nc.gpsimd
                variance(st, sm, n, sem_, v0)
                pool_.tensor_scalar(sm[:, 7, :], sm[:, 6, :], 1.0, eps, ALU.mult, ALU.add).then_inc(sem_, 1)
                pool_.tensor_scalar(sm[:, 8, :], sm[:, 4, :], -0.5, 1.0, ALU.mult, ALU.mult).then_inc(sem_, 1)
                after(sem_, v0 + 9)
                pool_.tensor_tensor(rs, sm[:, 7, :], neg_half[:, 0:n], ALU.pow).then_inc(sem_, 1)
                after(sem_, v0 + 10)
                return pool_.tensor_tensor(nm, sm[:, 8, :], rs, ALU.mult)

            def body1(u, par, runs):
                if runs(1):
                    g, k = u - 1, (par - 1) % 2
                    after(a_stats, g + 1)
                    after(a_nv, T * (g - 2) + T)
                    after(a_na, T * (g - 2) + T)
                    rstd(st1[:, k], sm1, T * TOK, EPS_TOK, rs1[:, k, :], nm1[:, k, :], a_small, g * SMALL1
                         ).then_inc(a_coef, 1)
                    after(a_coef, g + 1)
                    for t in range(T):
                        for j in (1, 2):
                            ins = nc.gpsimd.tensor_scalar(
                                xs[:, k * T + t, j, :], xs[:, k * T + t, j, :],
                                rs1[:, k, t * TOK + j:t * TOK + j + 1], nm1[:, k, t * TOK + j:t * TOK + j + 1],
                                ALU.mult, ALU.add)
                        ins.then_inc(a_np, 1)
            groups(pool, body1, 2, 4, 2)

            def body2(u, par, runs):
                if runs(0):
                    g, k = u, par % 2
                    after(b_stats, g + 1)
                    after(b_xtr, g - 1)
                    rstd(st2[:, k], sm2, T, EPS, rs2[:, k, :], nm2[:, k, :], b_small, g * SMALL2).then_inc(b_small, 1)
                    after(b_small, g * SMALL2 + 11)
                    bc = lambda a: a.unsqueeze(2).to_broadcast([P, T, D])
                    nc.gpsimd.tensor_tensor(xn[:, k, :, :], tok_out[:, bass.ds(g * T, T), :], bc(rs2[:, k, :]), ALU.mult
                                            ).then_inc(b_small, 1)
                    after(b_small, g * SMALL2 + 12)
                    nc.gpsimd.tensor_tensor(xn[:, k, :, :], xn[:, k, :, :], bc(nm2[:, k, :]), ALU.add).then_inc(b_xn, 1)
                if runs(S1):
                    g = u - S1
                    v = 4 * g
                    after(b_cbf, g + 1)
                    after(b_cbtr, g)
                    nc.gpsimd.tensor_copy(cb3[:, 0, :], cbf[:, :]).then_inc(b_cbs, 1)
                    after(b_cbs, v + 1)
                    nc.gpsimd.tensor_tensor(cbr[:, :], cbf[:, :], cb3[:, 0, :], ALU.subtract).then_inc(b_cbs, 1)
                    after(b_cbs, v + 2)
                    nc.gpsimd.tensor_copy(cb3[:, 1, :], cbr[:, :]).then_inc(b_cbs, 1)
                    after(b_cbs, v + 3)
                    nc.gpsimd.tensor_tensor(cb3[:, 2, :], cbr[:, :], cb3[:, 1, :], ALU.subtract).then_inc(b_cbs, 1)
                if runs(S4):
                    g, k, kr = u - S4, (par - S4) % 2, (par - S4) % 4
                    v = SMALL3 * g
                    after(c_stats, g + 1)
                    variance(st3[:, k], sm3, T, c_small, v)
                    p_ = nc.gpsimd
                    p_.tensor_scalar(sm3[:, 7, :], sm3[:, 6, :], 1.0, EPS, ALU.mult, ALU.add).then_inc(c_small, 1)
                    p_.tensor_scalar(sm3[:, 8, :], sm3[:, 4, :], -0.5, 1.0, ALU.mult, ALU.mult).then_inc(c_small, 1)
                    after(c_small, v + 9)
                    p_.tensor_tensor(sm3[:, 9, :], sm3[:, 7, :], neg_half[:, 0:T], ALU.pow).then_inc(c_small, 1)
                    after(c_small, v + 10)
                    p_.tensor_tensor(sm3[:, 10, :], sm3[:, 9, :], sm3[:, 9, :], ALU.mult).then_inc(c_small, 1)
                    p_.tensor_tensor(sm3[:, 11, :], sm3[:, 8, :], sm3[:, 9, :], ALU.mult).then_inc(c_small, 1)
                    after(c_small, v + 12)
                    p_.tensor_tensor(sm3[:, 12, :], sm3[:, 6, :], sm3[:, 10, :], ALU.mult).then_inc(c_small, 1)
                    after(c_small, v + 13)
                    p_.tensor_scalar(sm3[:, 13, :], sm3[:, 12, :], 1.0, EPS, ALU.mult, ALU.add).then_inc(c_small, 1)
                    after(c_small, v + 14)
                    p_.tensor_tensor(sm3[:, 14, :], sm3[:, 13, :], neg_half[:, 0:T], ALU.pow).then_inc(c_small, 1)
                    after(c_small, v + 15)
                    p_.tensor_tensor(row[:, kr, :, SCALE], sm3[:, 9, :], sm3[:, 14, :], ALU.mult).then_inc(c_small, 1)
                    after(c_small, v + 16)
                    p_.tensor_tensor(row[:, kr, :, SHIFT], sm3[:, 8, :], row[:, kr, :, SCALE], ALU.mult).then_inc(c_small, 1)
                    p_.tensor_copy(row[:, kr, :, TOKEN].bitcast(I32),
                                   cint[:, bass.ds(g * T, T)]).then_inc(c_small, 1)
                    after(c_xtr, g - 1)
                    for t in range(T):
                        ins = p_.tensor_scalar(xg[:, k, t, :], row[:, kr, t, 0:D], sm3[:, 9, t:t + 1],
                                               sm3[:, 11, t:t + 1], ALU.mult, ALU.add)
                    ins.then_inc(c_xg, 1)
                if runs(S6):
                    g, k = u - S6, (par - S6) % 4
                    after(c_rt, ROUTE * g + ROUTE)
                    after(c_small, SMALL3 * (g + 1))
                    for t in range(T):
                        nc.gpsimd.indirect_dma_start(
                            out=rows[:, :], out_offset=bass.IndirectOffsetOnAxis(ap=pos[:, k, t:t + 1], axis=0),
                            in_=row[:, k, t, :], in_offset=None).then_inc(c_scat[k], 16)
            groups(pool, body2, S6, 8, 4)

            def store(i, k, slot):
                after(e_o, i + 1)
                nc.gpsimd.indirect_dma_start(
                    out=out, out_offset=bass.IndirectOffsetOnAxis(ap=er[:, slot, TOKEN:TOKEN + 1].bitcast(I32), axis=0),
                    in_=eo[:, k, :], in_offset=None, bounds_check=N - 1, oob_is_err=False).then_inc(e_out[k], 16)
            for i in range(4):
                store(i, i % 2, i)
            with pool.Fori(0, NX // 4 - 1) as four:
                for c in range(4):
                    store(four * 4 + (4 + c), c % 2, c)
            for i in range(NX - (NX % 4), NX):
                store(i, i % 2, i % 4)
            after(e_out[0], 16 * ((NX + 1) // 2))
            after(e_out[1], 16 * (NX // 2))

        @block.scalar
        def _(act):
            act.dma_start(w_raw[:, :, :], w_tok.rearrange("(j e) o -> e j o", j=TOK)).then_inc(s_wtok, 16)
            act.dma_start(cols[:, 0:1], g_tok).then_inc(s_wtok, 16)
            act.dma_start(cols[:, 1:2], b_tok).then_inc(s_wtok, 16)
            act.dma_start(cols[:, 2:3], g_ffn).then_inc(s_wtok, 16)
            act.dma_start(bias_row[:, 0, :], bias_tok).then_inc(s_wtok, 16)
            act.dma_start(bias_row[:, 1, :], bd).then_inc(s_wtok, 16)
            for i, w in enumerate((wq_t, wk_t, wv_t, wd_t)):
                act.dma_start(wqkvd[:, i, :], w).then_inc(s_watt, 16)
            act.dma_start(wb_sb[:, :], wb_t).then_inc(s_watt, 16)
            act.dma_start(mix_sb[:, :], mix_t).then_inc(s_watt, 16)
            act.dma_start(wg_sb[:, :], w_gate).then_inc(s_watt, 16)

            def evac1(n, k):
                need(act, a_tr, n + 1)
                need(act, a_mm, n - 1)
                nc.scalar.activation(xt[:, k, :], bank[k][:, :], ACT.Copy).then_inc(a_ev, 1)

            def gelu1(g, k):
                need(act, a_mm, T * g + T)
                dst = tok_out[:, bass.ds(g * T, T), :]
                nc.scalar.activation(dst, bank[2 + k][:, :].rearrange("p (t d) -> p t d", t=T), ACT.Gelu).then_inc(a_out, 1)

            def body1(u, par, runs):
                g, k = u - 1, (par - 1) % 2
                if runs(1):
                    need(act, a_coef, g + 1)
                for t in range(T):
                    if runs(1):
                        j = 3
                        nc.scalar.activation(xs[:, k * T + t, j, :], xs[:, k * T + t, j, :], ACT.Identity,
                                             bias=nm1[:, k, t * TOK + j:t * TOK + j + 1],
                                             scale=rs1[:, k, t * TOK + j:t * TOK + j + 1]).then_inc(a_na, 1)
                    if (t > 0 and runs(1)) or (t == 0 and runs(2)):
                        evac1(g * T + t - 1, (t - 1) % 2)
                    if t == 1 and runs(2):
                        gelu1(g - 1, 1 - k)
            groups(act, body1, 2, 4, 2)

            def body2(u, par, runs):
                k1 = (par - S1) % 2
                for t in range(T):
                    s, tt = (S2, t - 1) if t else (S3, T - 1)
                    if runs(s):
                        n = (u - s) * T + tt
                        need(act, b_ptr, n + 1)
                        need(act, b_pv, n - 1)
                        nc.scalar.activation(pt[:, tt % 2, :, :].rearrange("p a b -> p (a b)"), bank[6 + tt % 2][:, :],
                                             ACT.Copy).then_inc(b_pt, 1)
                    g = u - S1
                    if t == 0 and runs(S1):
                        need(act, b_cb, g + 1)
                        need(act, b_cbs, 4 * g)
                        nc.scalar.activation(cbf[:, :], bank[2][:, 0:T * H], ACT.Copy).then_inc(b_cbf, 1)
                        need(act, b_q, g + 1)
                        need(act, b_sc, T * (g - 1))
                        nc.scalar.activation(qt[:, k1, :], bank[3][:, :], ACT.Copy).then_inc(b_qt, 1)
                        need(act, b_k, g + 1)
                        need(act, b_kmv, g - 1)
                        nc.scalar.activation(kt[:, k1, :], bank[2][:, :], ACT.Copy).then_inc(b_kt, 1)
                    if t == 1 and runs(S1):
                        need(act, b_v, 2 * g + 1)
                        need(act, b_pv, T * (g - 1))
                        src = bank[3][:, :].rearrange("p (b h d) -> p b h d", b=T, h=HP)
                        nc.scalar.activation(vb[0:64, k1, 0:T, :, 0:DH], src[0:64, :, :, 0:DH], ACT.Copy)
                        nc.scalar.activation(vb[64:128, k1, 0:T, :, VW:VW + DH], src[64:128, :, :, DH:2 * DH],
                                             ACT.Copy).then_inc(b_va, 1)
                        act.wait_ge(b_kt, g + 1)
                    if t in (1, 2, 3) and runs(S1):
                        h = 4 + t
                        ins = nc.scalar.activation(kmix[:, k1, h, :], kt[:, k1, :], ACT.Copy, scale=mix_sb[:, h:h + 1])
                        if t == 3:
                            ins.then_inc(b_kma, 1)
                    if t == 2 and runs(S1):
                        need(act, b_cbtr, g + 1)
                        if runs(S2):
                            kk = (par - S2) % 2
                            gg = u - S2
                            if isinstance(gg, int):
                                act.wait_ge(b_cbrow[kk], 96 * (gg // 2 + 1))
                            else:
                                act.wait_ge(b_cbrow[kk], (gg - kk) * 48 + 96)
                        nc.scalar.activation(cbt[:, :], bank[2][0:96, 0:64].bitcast(BF16), ACT.Copy).then_inc(b_cbt, 1)
                    if t == 2 and runs(S5):
                        g5 = u - S5
                        need(act, c_xtr, g5 + 1)
                        need(act, c_gate, g5)
                        nc.scalar.activation(xgt[:, :], bank[3][:, :], ACT.Copy).then_inc(c_xt, 1)
                    if t == 3 and runs(S3):
                        g3 = u - S3
                        need(act, c_tr, g3 + 1)
                        need(act, c_wd, g3)
                        nc.scalar.activation(ctxt[:, :], bank[2][:, :], ACT.Copy).then_inc(c_ct, 1)
                    if t == 1 and runs(S6):
                        g6 = u - S6
                        need(act, c_rt, ROUTE * g6 + 2)
                        nc.scalar.activation(rt[:, 1, :, :], rt[:, 0, :, :], ACT.Exp).then_inc(c_exp, 1)
                    if runs(S2):
                        n = (u - S2) * T + t
                        need(act, b_sub, n + 1)
                        need(act, b_ptr, n - 1)
                        nc.scalar.activation(pe_[:, t % 2, :], pr[:, t % 2, :, :].rearrange("p h s -> p (h s)"), ACT.Exp,
                                             scale=1.0 / float(D / H) ** 0.5).then_inc(b_exp, 1)
                    if t == 3 and runs(0):
                        need(act, b_xtr, u + 1)
                        need(act, b_v, 2 * (u - 1))
                        nc.scalar.activation(xnt[:, par % 2, :], bank[3][:, :], ACT.Copy).then_inc(b_xt, 1)
            act.wait_ge(s_watt, 16 * 7)
            groups(act, body2, S6, 8, 4)

            act.wait_ge(s_wexp, 32 * E)
            act.wait_ge(s_wtok, 16 * 6)
            def body3(i, on):
                if on(0):
                    need(act, e_tr, i + 1)
                    need(act, e_f1, i - 1)
                    nc.scalar.activation(ext[:, on.k(0), :], bank[0 + on.k(0)][:, 0:P], ACT.Copy).then_inc(e_xt, 1)
                if on(1):
                    need(act, e_f1, i)
                    need(act, e_htr, i - 2)
                    nc.scalar.activation(hid[:, on.k(1), :], bank[2 + on.k(1)][:, :], ACT.Gelu).then_inc(e_hid, 1)
            tiles3(act, body3, 3)

        @block.tensor
        def _(pe):
            mm = nc.tensor.matmul
            pe.wait_ge(s_set, 2)
            pe.wait_ge(s_wtok, 16 * 6)
            for j in range(TOK):
                mm(bank[0][:, 0:D], beta_bc[:, :], w_raw[:, j, :], start=(j == 0), stop=False)
            mm(bank[0][:, 0:D], cst[0:1, C_ONE:C_ONE + P], bias_row[:, 0, :], start=False, stop=True)
            mm(bank[1][:, 0:D], cst[0:1, C_ONE:C_ONE + P], bias_row[:, 1, :], start=True, stop=True).then_inc(s_bias_ps, 1)
            pe.wait_ge(s_set, 20)

            def bias(dst, i, last):
                mm(dst, sel_bf[:, :], bias3[:, i:i + 1, :].to_broadcast([P, T, D]), start=True, stop=last,
                   skip_group_check=True)

            def product1(g, t, k):
                n = g * T + t
                need(pe, a_ev, n + 1)
                if t == 0:
                    need(pe, a_out, g - 1)
                    bias(bank[2 + k][:, :].rearrange("p (t d) -> p t d", t=T), 0, False)
                for j in range(TOK):
                    ins = mm(bank[2 + k][:, t * D:(t + 1) * D], xt[:, t % 2, j * P:(j + 1) * P], w_sc[:, j, :],
                             start=False, stop=(j == TOK - 1 and t == T - 1), skip_group_check=True)
                ins.then_inc(a_mm, 1)

            def body1(u, par, runs):
                g, k = u - 1, (par - 1) % 2
                for t in range(T):
                    if runs(1):
                        n = g * T + t
                        need(pe, a_nv, n + 1)
                        need(pe, a_np, n + 1)
                        need(pe, a_na, n + 1)
                        need(pe, a_ev, n - 1)
                        for j in range(TOK):
                            ins = nc.tensor.transpose(bank[t % 2][:, j * P:(j + 1) * P], xs[:, k * T + t, j, :], ident)
                        ins.then_inc(a_tr, 1)
                    if t > 0 and runs(1):
                        product1(g, t - 1, k)
                    if t == 0 and runs(2):
                        product1(g - 1, T - 1, 1 - k)
            groups(pe, body1, 2, 4, 2)

            pe.wait_ge(a_out, NG)
            pe.wait_ge(s_watt, 16 * 7)
            pe.wait_ge(s_padr, 4)
            wq, wk, wv, wd = (wqkvd[:, i, :] for i in range(4))

            def body2(u, par, runs):
                g0, k0 = u, par % 2
                g1, k1 = u - S1, (par - S1) % 2
                g3, k3 = u - S3, (par - S3) % 2
                g4, k4 = u - S4, (par - S4) % 2
                g5, k5 = u - S5, (par - S5) % 2
                g6 = u - S6

                for t in range(T):
                    if runs(S2):
                        g, k = u - S2, (par - S2) % 2
                        n = g * T + t
                        if t == 0:
                            need(pe, b_kmv, g + 1)
                            need(pe, b_kma, g + 1)
                            if isinstance(g, int):
                                pe.wait_ge(b_cbrow[k], 96 * (g // 2 + 1))
                            else:
                                pe.wait_ge(b_cbrow[k], (g - k) * 48 + 96)
                        need(pe, b_sub, n - 1)
                        sc = bank[4 + t % 2]
                        for s in range(2):
                            c = t * P + s * SEQ
                            mm(sc[s * SEQ:(s + 1) * SEQ, :], qt[:, k, c:c + SEQ], kmix[:, k, :, c:c + SEQ],
                               start=True, stop=False, skip_group_check=True)
                        mm(sc[:, :], ind_bf[:, :], cbrow[:, k, t * H:(t + 1) * H, :], start=False, stop=True,
                           skip_group_check=True).then_inc(b_sc, 1)
                    s, tt = (S2, t - 1) if t else (S3, T - 1)
                    if runs(s):
                        n = (u - s) * T + tt
                        need(pe, b_exp, n + 1)
                        need(pe, b_pt, n - 1)
                        for hp in range(HP):
                            ins = nc.tensor.transpose(bank[6 + tt % 2][:, hp * P:(hp + 1) * P],
                                                      pe_[:, tt % 2, hp * P:(hp + 1) * P], ident)
                        ins.then_inc(b_ptr, 1)
                    s, tt = (S2, t - 2) if t > 1 else (S3, t + 2)
                    if runs(s):
                        g, k = u - s, (par - s) % 2
                        n = g * T + tt
                        need(pe, b_pt, n + 1)
                        if tt == 0:
                            need(pe, b_va, g + 1)
                            need(pe, b_vv, g + 1)
                        need(pe, b_cn, n - 1)
                        for hp in range(HP):
                            for q in range(2):
                                ins = mm(bank[tt % 2][q * SEQ:(q + 1) * SEQ, hp * 2 * VW:(hp + 1) * 2 * VW],
                                         pt[:, tt % 2, hp, q * SEQ:(q + 1) * SEQ], vb[:, k, 2 * tt + q, hp, :],
                                         start=True, stop=True, skip_group_check=True)
                        ins.then_inc(b_pv, 1)

                    if t == 0 and runs(S1):
                        need(pe, b_xt, g1 + 1)
                        if runs(S4):
                            need(pe, c_ct, g4 + 1)
                        else:
                            need(pe, b_cbt, g1)
                        for i in range(T):
                            ins = mm(bank[2][:, i * H:(i + 1) * H], xnt[:, k1, i * P:(i + 1) * P], wb_sb[:, :],
                                     start=True, stop=True, skip_group_check=True)
                        ins.then_inc(b_cb, 1)
                        mm(bank[3][:, :], wq, xnt[:, k1, :], start=True, stop=True).then_inc(b_q, 1)
                        need(pe, b_cbf, g1 + 1)
                        mm(bank[2][:, :], wk, xnt[:, k1, :], start=True, stop=True).then_inc(b_k, 1)
                    if t == 1 and runs(S1):
                        for i in range(2):
                            need(pe, b_kt if i else b_qt, g1 + 1)
                            for b in range(T):
                                c = (i * T + b) * SEQ
                                for half in range(2):
                                    ins = mm(bank[3 - i][half * 64:(half + 1) * 64, b * D:(b + 1) * D],
                                             xnt[:, k1, c:c + SEQ], wv, start=True, stop=True, skip_group_check=True)
                            ins.then_inc(b_v, 1)
                    if t == 1 and runs(S4):
                        need(pe, c_ct, g4 + 1)
                        if runs(S1):
                            need(pe, b_va, g1 + 1)
                        else:
                            need(pe, c_rt, ROUTE * g6 + 2)
                        bias(bank[3][:, :].rearrange("p (t d) -> p t d", t=T), 1, False)
                        for i in range(T):
                            ins = mm(bank[3][:, i * D:(i + 1) * D], ctxt[:, i * P:(i + 1) * P], wd, start=False,
                                     stop=(i == T - 1), skip_group_check=True)
                        ins.then_inc(c_wd, 1)
                    if t == 2 and runs(S1):
                        need(pe, b_cbs, 4 * g1 + 4)
                        need(pe, b_vv, g1 + 1)
                        nc.tensor.transpose(bank[2][0:96, 0:64].bitcast(BF16), cb3[:, :, :].rearrange("p a b -> p (a b)"),
                                            ident_bf[:, :]).then_inc(b_cbtr, 1)
                    if t == 2 and runs(S5):
                        need(pe, c_xg, g5 + 1)
                        if runs(S4):
                            need(pe, c_res, g4 + 1)
                        else:
                            need(pe, c_res, NG)
                            need(pe, c_rt, ROUTE * g6 + 2)
                        for i in range(T):
                            ins = nc.tensor.transpose(bank[3][:, i * P:(i + 1) * P], xg[:, k5, i, :], ident)
                        ins.then_inc(c_xtr, 1)
                    if t == 2 and runs(S6):
                        need(pe, c_rt, ROUTE * g6 + 13)
                        if runs(S1):
                            need(pe, b_cbt, g1 + 1)
                        else:
                            need(pe, b_cbt, NG)
                            need(pe, c_ct, u - S4 + 1 if runs(S4) else NG)
                        o = oh_bf[:, :, :].rearrange("p t e -> p (t e)")
                        mm(bank[2][:, 0:T * E], tri_bf[:, :], o, start=True, stop=False, skip_group_check=True)
                        for i in range(T):
                            ins = mm(bank[2][:, (i + 1) * E:(T + 1) * E], ones_bf[:, :], o[:, 0:(T - i) * E],
                                     start=False, stop=(i == T - 1), skip_group_check=True)
                        ins.then_inc(c_pre, 1)
                    if t == 3 and runs(S5):
                        need(pe, c_xt, g5 + 1)
                        for i in range(T):
                            ins = mm(bank[3][:, i * E:(i + 1) * E], xgt[:, i * P:(i + 1) * P], wg_sb[:, :],
                                     start=True, stop=True, skip_group_check=True)
                        ins.then_inc(c_gate, 1)
                    if t == 3 and runs(S3):
                        need(pe, b_cn, T * g3 + T)
                        if runs(S6):
                            need(pe, c_rt, ROUTE * g6 + 15)
                        elif runs(S1):
                            need(pe, b_cbt, g1 + 1)
                        for i in range(T):
                            ins = nc.tensor.transpose(bank[2][:, i * P:(i + 1) * P], ctxn[:, k3, i, :], ident)
                        ins.then_inc(c_tr, 1)
                    if t == 3 and runs(0):
                        need(pe, b_xn, g0 + 1)
                        if runs(S5):
                            need(pe, c_rt, ROUTE * g5 + 2)
                        elif runs(S4):
                            need(pe, c_res, g4 + 1)
                        elif runs(S1):
                            need(pe, b_va, g1 + 1)
                        for i in range(T):
                            ins = nc.tensor.transpose(bank[3][:, i * P:(i + 1) * P], xn[:, k0, i, :], ident)
                        ins.then_inc(b_xtr, 1)
            groups(pe, body2, S6, 8, 4)

            pe.wait_ge(s_w1s, E)
            pe.wait_ge(s_wexp, 32 * E)
            pe.wait_ge(s_tab, 20)
            pe.wait_ge(c_rt, ROUTE * NG)

            def body3(i, on):
                if on(0):
                    need(pe, e_n, i + 1)
                    need(pe, e_xt, i - 1)
                    nc.tensor.transpose(bank[on.k(0)][:, 0:P], ex[:, on.k(0), :], ident).then_inc(e_tr, 1)
                if on(1):
                    e = pe.value_load(ti[0:1, 1, bass.ds(i - 1, 1)], min_val=0, max_val=E - 1)
                    need(pe, e_xt, i)
                    need(pe, e_hid, i - 2)
                    mm(bank[2 + on.k(1)][:, :], ext[:, on.k(1), :], w1_sb[:, bass.ds(e, 1), :], start=True, stop=True
                       ).then_inc(e_f1, 1)
                if on(2):
                    need(pe, e_hid, i - 1)
                    need(pe, e_ht, i - 3)
                    for c in range(HC):
                        ins = nc.tensor.transpose(bank[4 + on.k(2)][:, c * P:(c + 1) * P],
                                                  hid[:, on.k(2), c * P:(c + 1) * P], ident)
                    ins.then_inc(e_htr, 1)
                if on(3):
                    e = pe.value_load(ti[0:1, 1, bass.ds(i - 3, 1)], min_val=0, max_val=E - 1)
                    need(pe, e_ht, i - 2)
                    need(pe, e_o, i - 4)
                    for c in range(HC):
                        ins = mm(bank[6 + on.k(3)][:, 0:D], hidt[:, on.k(3), c, :], w2_sb[:, bass.ds(e, 1), c, :],
                                 start=(c == 0), stop=(c == HC - 1))
                    ins.then_inc(e_f2, 1)
            tiles3(pe, body3, 3)

        @block.vector
        def _(dve):
            v_ = nc.vector
            def step(ins, n):
                ins.then_inc(s_set, 1)
                dve.wait_ge(s_set, n)
            dve.wait_ge(s_cst, 32)
            dve.wait_ge(s_wtok, 16 * 6)
            step(v_.tensor_scalar(beta_bc[:, :], cst[:, C_ONE:C_ONE + P], cols[:, 1:2], None, ALU.mult), 1)
            step(v_.tensor_copy(ident_bf[:, :], ident), 2)
            step(v_.tensor_copy(tri_bf[:, :], cst[:, C_TRI:C_TRI + P]), 3)
            step(v_.tensor_copy(ones_bf[:, :], cst[:, C_ONE:C_ONE + P]), 4)
            step(v_.tensor_copy(ind_bf[:, :], cst[:, C_IND:C_IND + P]), 5)
            step(v_.tensor_copy(sel_bf[:, :], cst[:, C_SEL:C_SEL + P]), 6)
            step(v_.tensor_scalar(w_sc[:, :, :], w_raw[:, :, :], cols[:, 0:1], None, ALU.mult), 7)
            step(v_.memset(bias3[:, :, :], 0.0), 8)
            dve.wait_ge(s_bias_ps, 1)
            step(v_.tensor_copy(bias_f[:, 0, :], bank[0][:, 0:D]), 9)
            step(v_.tensor_copy(bias_f[:, 1, :], bank[1][:, 0:D]), 10)
            step(v_.tensor_copy(bias_hi[:, :, :], bias_f[:, :, :]), 11)
            step(v_.tensor_tensor(bias_r[:, :, :], bias_f[:, :, :], bias_hi[:, :, :], ALU.subtract), 12)
            step(v_.tensor_copy(bias_mid[:, :, :], bias_r[:, :, :]), 13)
            step(v_.tensor_tensor(bias_lo[:, :, :], bias_r[:, :, :], bias_mid[:, :, :], ALU.subtract), 14)
            step(v_.tensor_copy(bias3[0:32, :, :], bias_hi[0:32, :, :]), 15)
            step(v_.tensor_copy(bias3[32:64, :, :], bias_mid[32:64, :, :]), 16)
            step(v_.tensor_copy(bias3[64:96, :, :], bias_lo[64:96, :, :]), 17)
            step(v_.tensor_copy(base[:, :], cst[:, C_BASE:C_BASE + E]), 18)
            step(v_.memset(vb[:, :, :, :, :], 0.0), 19)
            v_.memset(vb[0:64, :, :, :, DH:DH + 1], 1.0)
            step(v_.memset(vb[64:128, :, :, :, 2 * VW - 1:2 * VW], 1.0), 20)

            def body1(u, par, runs):
                for t in range(T):
                    if runs(0):
                        slot = par * T + t
                        if isinstance(u, int):
                            dve.wait_ge(x_in[slot], 16 * (u // 2 + 1))
                        else:
                            dve.wait_ge(x_in[slot], (u - par) * 8 + 16)
                        if t == 0:
                            need(dve, a_coef, u - 1)
                        for j in range(TOK):
                            ins = v_.bn_stats(st1[:, par, t * TOK + j, :], xs[:, slot, j, :])
                        if t == T - 1:
                            ins.then_inc(a_stats, 1)
                    if runs(1):
                        g, k = u - 1, (par - 1) % 2
                        if t == 0:
                            need(dve, a_coef, g + 1)
                        v_.tensor_scalar(xs[:, k * T + t, 0, :], xs[:, k * T + t, 0, :], rs1[:, k, t * TOK:t * TOK + 1],
                                         nm1[:, k, t * TOK:t * TOK + 1], ALU.mult, ALU.add).then_inc(a_nv, 1)
            groups(dve, body1, 2, 4, 2)

            dve.wait_ge(s_watt, 16 * 7)

            def route(g, kr, part):
                v = ROUTE * g
                iota = cst[:, C_IOTA:C_IOTA + T * E].rearrange("p (t e) -> p t e", t=T)
                s_, r_ = bank[3][:, 0:T * E].rearrange("p (t e) -> p t e", t=T), rt
                bc = lambda a: a.unsqueeze(2).to_broadcast([P, T, E])

                def step(ins, n):
                    ins.then_inc(c_rt, 1)
                    dve.wait_ge(c_rt, v + n)

                if part == 0:
                    need(dve, c_gate, g + 1)
                    step(v_.tensor_reduce(r4[:, 0, :], s_, X, ALU.max), 1)
                    step(v_.tensor_tensor(rt[:, 0], s_, bc(r4[:, 0, :]), ALU.subtract), 2)
                if part == 1:
                    need(dve, c_exp, g + 1)
                    step(v_.tensor_reduce(r4[:, 1, :], rt[:, 1], X, ALU.add), 3)
                    step(v_.reciprocal(r4[:, 2, :], r4[:, 1, :]), 4)
                    step(v_.tensor_tensor(rt[:, 2], rt[:, 1], bc(r4[:, 2, :]), ALU.mult), 5)
                    step(v_.tensor_reduce(r4[:, 3, :], rt[:, 2], X, ALU.max), 6)
                    step(v_.tensor_tensor(rt[:, 3], rt[:, 2], bc(r4[:, 3, :]), ALU.is_equal), 7)
                    step(v_.tensor_tensor(rt[:, 4], rt[:, 3], iota, ALU.mult), 8)
                    step(v_.tensor_reduce(r4[:, 4, :], rt[:, 4], X, ALU.min), 9)
                    step(v_.tensor_tensor(rt[:, 5], iota, bc(r4[:, 4, :]), ALU.is_equal), 10)
                    step(v_.tensor_tensor(rt[:, 6], rt[:, 2], rt[:, 5], ALU.mult), 11)
                    step(v_.tensor_tensor(rt[:, 7], rt[:, 2], rt[:, 6], ALU.subtract), 12)
                    step(v_.tensor_copy(oh_bf[:, :, :], rt[:, 5]), 13)
                if part == 2:
                    need(dve, c_pre, g + 1)
                    step(v_.tensor_tensor(rt[:, 8], bank[2][:, 0:T * E].rearrange("p (t e) -> p t e", t=T),
                                          base[:, :].unsqueeze(1).to_broadcast([P, T, E]), ALU.add), 14)
                    step(v_.tensor_tensor(base[:, :], bank[2][:, T * E:(T + 1) * E], base[:, :], ALU.add), 15)
                    step(v_.tensor_tensor(rt[:, 9], rt[:, 8], rt[:, 5], ALU.mult), 16)
                    step(v_.tensor_reduce(r4[:, 5, :], rt[:, 9], X, ALU.add), 17)
                    v_.tensor_copy(pos[:, kr, :], r4[:, 5, :]).then_inc(c_rt, 1)
                    step(v_.tensor_reduce(r4[:, 6, :], rt[:, 7], X, ALU.max), 19)
                    step(v_.scalar_tensor_tensor(r4[:, 7, :], r4[:, 3, :], 1e-9, r4[:, 6, :], ALU.add, ALU.add), 20)
                    step(v_.reciprocal(r4[:, 8, :], r4[:, 7, :]), 21)
                    step(v_.tensor_tensor(row[:, kr, :, GATE], r4[:, 3, :], r4[:, 8, :], ALU.mult), 22)

            def sent(g, kr):
                return g // 4 * 16 * T if isinstance(g, int) else (g - kr) * (4 * T)

            def body2(u, par, runs):
                k1 = (par - S1) % 2
                g1 = u - S1
                for t in range(T):
                    if runs(S2):
                        n = (u - S2) * T + t
                        need(dve, b_sc, n + 1)
                        sc = bank[4 + t % 2][:, :].rearrange("p (h s) -> p h s", h=H)
                        v_.tensor_reduce(mx[:, t % 2, :], sc, X, ALU.max).then_inc(b_mx, 1)
                        dve.wait_ge(b_mx, n + 1)
                        need(dve, b_exp, n - 1)
                        v_.tensor_tensor(pr[:, t % 2, :, :], sc, mx[:, t % 2, :].unsqueeze(2).to_broadcast([P, H, SEQ]),
                                         ALU.subtract).then_inc(b_sub, 1)
                    if t == 0 and runs(0):
                        need(dve, a_out, u + 1)
                        need(dve, b_xn, u - 1)
                        for i in range(T):
                            src = tile(u * T + i)
                            ins = v_.bn_stats(st2[:, par % 2, i, :], src)
                        ins.then_inc(b_stats, 1)
                    if t == 1 and runs(S6):
                        route(u - S6, (par - S6) % 4, 1)
                    if t == 1 and runs(S1):
                        need(dve, b_kt, g1 + 1)
                        need(dve, b_v, 2 * g1 + 2)
                        need(dve, b_pv, T * (g1 - 1))
                        src = bank[2][:, :].rearrange("p (b h d) -> p b h d", b=T, h=HP)
                        v_.tensor_copy(vb[0:64, k1, T:2 * T, :, 0:DH], src[0:64, :, :, 0:DH])
                        v_.tensor_copy(vb[64:128, k1, T:2 * T, :, VW:VW + DH], src[64:128, :, :, DH:2 * DH]).then_inc(b_vv, 1)
                    if t in (1, 2, 3) and runs(S1):
                        for h in ((0,), (1, 2), (3, 4))[t - 1]:
                            ins = v_.tensor_scalar(kmix[:, k1, h, :], kt[:, k1, :], mix_sb[:, h:h + 1], None, ALU.mult)
                        if t == 3:
                            ins.then_inc(b_kmv, 1)
                    s, tt = (S2, t - 2) if t > 1 else (S3, t + 2)
                    if runs(s):
                        g, k = u - s, (par - s) % 2
                        n = g * T + tt
                        need(dve, b_pv, n + 1)
                        cp = bank[tt % 2][:, 0:H * VW].rearrange("p (a b c) -> p a b c", a=HP, b=2)
                        v_.reciprocal(rden[:, tt % 2, :, :], cp[:, :, :, DH]).then_inc(b_rd, 1)
                        dve.wait_ge(b_rd, n + 1)
                        if tt == 0:
                            need(dve, c_tr, g - 1)
                        v_.tensor_tensor(ctxn[:, k, tt, :].rearrange("p (a b c) -> p a b c", a=HP, b=2), cp[:, :, :, 0:DH],
                                         rden[:, tt % 2, :, :].unsqueeze(3).to_broadcast([P, HP, 2, DH]),
                                         ALU.mult).then_inc(b_cn, 1)
                    if t == 2 and runs(S4):
                        g, k, kr = u - S4, (par - S4) % 2, (par - S4) % 4
                        need(dve, c_wd, g + 1)
                        need(dve, c_scat[kr], sent(g, kr))
                        src = tok_out[:, bass.ds(g * T, T), :]
                        v_.tensor_tensor(row[:, kr, :, 0:D], bank[3][:, :].rearrange("p (t d) -> p t d", t=T), src,
                                         ALU.add).then_inc(c_res, 1)
                        dve.wait_ge(c_res, g + 1)
                        for i in range(T):
                            ins = v_.bn_stats(st3[:, k, i, :], row[:, kr, i, 0:D])
                        ins.then_inc(c_stats, 1)
                    if t == 3 and runs(S6):
                        route(u - S6, (par - S6) % 4, 2)
                    if t == 3 and runs(S5):
                        route(u - S5, (par - S5) % 4, 0)
            groups(dve, body2, S6, 8, 4)

            dve.wait_ge(s_wexp, 32 * E)

            def tab(ins, n):
                ins.then_inc(s_tab, 1)
                dve.wait_ge(s_tab, n)
            cb_ = cst[0:1, C_BASE:C_BASE + E]
            tab(v_.tensor_copy(tei[:, 0, :], base[0:1, :]), 1)
            tab(v_.scalar_tensor_tensor(te[:, 0, :], base[0:1, :], float(P - 1), cb_, ALU.add, ALU.subtract), 2)
            tab(v_.tensor_copy(tei[:, 1, :], te[:, 0, :]), 3)
            tab(v_.tensor_scalar(tei[:, 1, :], tei[:, 1, :], 7, None, ALU.arith_shift_right), 4)
            tab(v_.tensor_copy(te[:, 1, :], tei[:, 1, :]), 5)
            tab(v_.tensor_copy(te[:, 2, :], te[:, 1, :]), 6)
            for e in range(1, E):
                tab(v_.tensor_tensor(te[:, 2, e:e + 1], te[:, 2, e - 1:e], te[:, 1, e:e + 1], ALU.add), 6 + e)
            tiles_i = cst[0:1, C_TILE:C_END].rearrange("p (i e) -> p i e", e=E)
            tab(v_.tensor_tensor(tg[:, 0], tiles_i, te[:, 2, :].unsqueeze(1).to_broadcast([1, NX, E]), ALU.is_ge), 12)
            tab(v_.tensor_tensor(tg[:, 1], tg[:, 0], te[:, 1, :].unsqueeze(1).to_broadcast([1, NX, E]), ALU.mult), 13)
            tab(v_.tensor_reduce(tn[:, 0, :], tg[:, 0], X, ALU.add), 14)
            tab(v_.tensor_reduce(tn[:, 1, :], tg[:, 1], X, ALU.add), 15)
            tab(v_.tensor_tensor(tn[:, 2, :], tiles_i[:, :, 0], tn[:, 1, :], ALU.subtract), 16)
            tab(v_.tensor_scalar(tn[:, 2, :], tn[:, 2, :], float(P), None, ALU.mult), 17)
            tab(v_.scalar_tensor_tensor(tn[:, 3, :], tn[:, 0, :], float(REGION), tn[:, 2, :], ALU.mult, ALU.add), 18)
            tab(v_.tensor_copy(ti[:, 0, :], tn[:, 3, :]), 19)
            tab(v_.tensor_scalar(ti[:, 1, :], tn[:, 0, :], float(E - 1), None, ALU.min), 20)
            for e in range(E):
                v_.tensor_scalar(w1_sb[:, e, :], w1_sb[:, e, :], cols[:, 2:3], None, ALU.mult).then_inc(s_w1s, 1)

            def body3(i, on):
                if on(0):
                    dve.wait_ge(e_in[on.slot(0)], 16 * (i // 4 + 1) if isinstance(i, int) else (i - on.c) * 4 + 16)
                    need(dve, e_tr, i - 1)
                    r = er[:, on.slot(0), :]
                    v_.tensor_scalar(ex[:, on.k(0), :], r[:, 0:D], r[:, SCALE:SCALE + 1], r[:, SHIFT:SHIFT + 1],
                                     ALU.mult, ALU.add).then_inc(e_n, 1)
                if on(2):
                    need(dve, e_htr, i - 1)
                    need(dve, e_f2, i - 3)
                    v_.tensor_copy(hidt[:, on.k(2), :, :].rearrange("p c t -> p (c t)"), bank[4 + on.k(2)][:, :]
                                   ).then_inc(e_ht, 1)
                if on(3):
                    need(dve, e_f2, i - 2)
                    if not (isinstance(i, int) and i < 5):
                        need(dve, e_out[on.k(3)], stored(i - 5, on.k(3)))
                    r = er[:, on.slot(3), :]
                    v_.scalar_tensor_tensor(eo[:, on.k(3), :], bank[6 + on.k(3)][:, 0:D], r[:, GATE:GATE + 1], r[:, 0:D],
                                            ALU.mult, ALU.add).then_inc(e_o, 1)
            tiles3(dve, body3, 3)


_OUT = (P, SEQ, D)


def kernel(x, L0_tok_ln_gamma, L0_tok_ln_beta, L0_tok_W, L0_tok_b, L0_attn_Wq, L0_attn_Wk, L0_attn_Wv, L0_attn_Wb,
           L0_attn_mixing, L0_attn_Wd, L0_attn_bd, L0_ffn_w_gating, L0_ffn_gamma, L0_ffn_w1, L0_ffn_w2):
    import concourse.bacc as bacc
    from concourse.bass_utils import run_bass_kernel_spmd

    c, i = constants()
    arrays = {
        "x": x, "w_tok": L0_tok_W, "g_tok": np.reshape(L0_tok_ln_gamma, (D, 1)), "b_tok": np.reshape(L0_tok_ln_beta, (D, 1)),
        "bias_tok": np.reshape(L0_tok_b, (1, D)), "wq_t": np.transpose(L0_attn_Wq), "wk_t": np.transpose(L0_attn_Wk),
        "wv_t": np.transpose(L0_attn_Wv), "wb_t": np.transpose(L0_attn_Wb), "mix_t": np.transpose(L0_attn_mixing),
        "wd_t": np.transpose(L0_attn_Wd), "bd": np.reshape(L0_attn_bd, (1, D)), "w_gate": L0_ffn_w_gating,
        "g_ffn": np.reshape(L0_ffn_gamma, (D, 1)), "w1": L0_ffn_w1, "w2": L0_ffn_w2, "cf": c, "ci": i,
    }
    arrays = {f"in_{n}": np.ascontiguousarray(a) for n, a in arrays.items()}
    nc = bacc.Bacc("TRN2", target_bir_lowering=False, num_devices=1)
    args = [nc.dram_tensor(n, a.shape, mybir.dt.from_np(a.dtype), kind="ExternalInput").ap() for n, a in arrays.items()]
    rows = nc.dram_tensor("rows", ((E * REGION + SPARE * P), ROWW), F32).ap()
    out = nc.dram_tensor("out", (N, D), F32, kind="ExternalOutput").ap()
    build(nc, *args, rows, out)
    r = run_bass_kernel_spmd(nc, [arrays], core_ids=[0])
    return np.reshape(r.results[0]["out"], _OUT)
```

```python
from contextlib import ExitStack

import numpy as np

import concourse.bass as bass
from concourse import mybir

F32 = mybir.dt.float32
BF16 = mybir.dt.bfloat16
I32 = mybir.dt.int32
ALU = mybir.AluOpType
ACT = mybir.ActivationFunctionType
X = mybir.AxisListType.X

P = 128
D = 128
TOK = 4
SEQ = 64
H = 8
DH = D // H
HP = H // 2
VW = DH + 1
PV_END = H * VW
E = 6
HID = 512
HC = HID // P
N = 8192
NT = N // P
T = 4
NG = NT // T
REGION = N + P
NX = E - 1 + -(-(N - (E - 1)) // P)
SPARE = NX - NT + 1
ROWW = 132
GATE, TOKEN, SCALE, SHIFT = 128, 129, 130, 131
EPS_TOK, EPS = 1e-6, 1e-5

C_ID, C_TRI, C_ONE, C_IND, C_SEL, C_IOTA, C_BASE, C_HALF, C_TILE = 0, 128, 256, 384, 512, 640, 664, 672, 688
C_END = C_TILE + NX * E


def constants():
    c = np.zeros((P, C_END), np.float32)
    p = np.arange(P)
    c[:, C_ID:C_ID + P] = np.eye(P)
    c[:, C_TRI:C_TRI + P] = p[:, None] < p[None, :]
    c[:, C_ONE:C_ONE + P] = 1.0
    for r in range(6):
        c[r, C_IND + SEQ * (r % 2):C_IND + SEQ * (r % 2) + SEQ] = 1.0
    c[0:96:32, C_SEL:C_SEL + P] = 1.0
    c[:, C_IOTA:C_IOTA + T * E] = np.tile(np.arange(E) - 8.0, T)
    c[:, C_BASE:C_BASE + E] = np.arange(E) * REGION
    c[:, C_HALF:C_HALF + 16] = -0.5
    c[:, C_TILE:C_END] = np.repeat(np.arange(NX), E)
    i = np.zeros((P, NT + 1), np.int32)
    i[:, 0:NT] = p[:, None] + P * np.arange(NT)[None, :]
    i[:, NT] = N + p
    return c, i


def need(eng, sem, value):
    if not isinstance(value, int) or value > 0:
        eng.wait_ge(sem, value)


def build(nc, x, w_tok, g_tok, b_tok, bias_tok, wq_t, wk_t, wv_t, wb_t, mix_t, wd_t, bd, w_gate, g_ffn, w1, w2,
          cf, ci, rows, out):
    ctx = ExitStack()
    with ctx:
        def sb(name, shape, dt=F32):
            return ctx.enter_context(nc.sbuf_tensor(name, shape, dt))

        def sem(name):
            return ctx.enter_context(nc.semaphore(name))

        bank = [ctx.enter_context(nc.psum_tensor(f"bank{i}", [P, 512], F32)) for i in range(8)]

        cst = sb("cst", [P, C_END])
        cint = sb("cint", [P, NT + 1], I32)
        ident = cst[:, C_ID:C_ID + P]
        neg_half = cst[:, C_HALF:C_HALF + 16]
        ident_bf = sb("ident_bf", [P, P], BF16)
        tri_bf = sb("tri_bf", [P, P], BF16)
        ones_bf = sb("ones_bf", [P, P], BF16)
        ind_bf = sb("ind_bf", [P, P], BF16)
        sel_bf = sb("sel_bf", [P, P], BF16)
        w_raw = sb("w_raw", [P, TOK, D])
        w_sc = sb("w_sc", [P, TOK, D])
        cols = sb("cols", [P, 4])
        beta_bc = sb("beta_bc", [P, P])
        bias_row = sb("bias_row", [1, 2, D])
        bias_f = sb("bias_f", [P, 2, D])
        bias_hi = sb("bias_hi", [P, 2, D], BF16)
        bias_r = sb("bias_r", [P, 2, D])
        bias_mid = sb("bias_mid", [P, 2, D], BF16)
        bias_lo = sb("bias_lo", [P, 2, D], BF16)
        bias3 = sb("bias3", [P, 2, D], BF16)
        wqkvd = sb("wqkvd", [P, 4, D])
        wb_sb = sb("wb_sb", [P, H])
        mix_sb = sb("mix_sb", [P, H])
        wg_sb = sb("wg_sb", [P, E])
        w1_sb = sb("w1_sb", [P, E, HID])
        w2_sb = sb("w2_sb", [P, E, HC, D])
        tok_out = sb("tok_out", [P, NT, D])
        xs = sb("xs", [P, 4 * T, TOK, D])
        st1 = sb("st1", [P, 2, T * TOK, 6])
        sm1 = sb("sm1", [P, 10, T * TOK])
        rs1 = sb("rs1", [P, 2, T * TOK])
        nm1 = sb("nm1", [P, 2, T * TOK])
        xt = sb("xt", [P, 2, TOK * P])
        x_flat = xs[:, :, :, :].rearrange("p a j e -> p (a j e)")
        st2 = sb("st2", [P, 2, T, 6])
        sm2 = sb("sm2", [P, 10, T])
        rs2 = sb("rs2", [P, 2, T])
        nm2 = sb("nm2", [P, 2, T])
        xn = sb("xn", [P, 2, T, D])
        xnt = sb("xnt", [P, 2, T * P])
        qt = sb("qt", [P, 2, T * P])
        kt = sb("kt", [P, 2, T * P])
        kmix = x_flat.rearrange("p (k h c) -> p k h c", k=2, h=H)
        vb = sb("vb", [P, 2, 2 * T, HP, 2 * VW])
        cbf = sb("cbf", [P, T * H])
        cbr = sb("cbr", [P, T * H])
        cb3 = sb("cb3", [P, 3, T * H], BF16)
        cbt = sb("cbt", [96, P], BF16)
        cbrow = sb("cbrow", [P, 2, T * H, SEQ], BF16)
        mx = sb("mx", [P, 2, H])
        pr = sb("pr", [P, 2, H, SEQ])
        pe_ = sb("pe_", [P, 2, H * SEQ])
        pt = sb("pt", [P, 2, HP, P])
        rden = sb("rden", [P, 2, HP, 2])
        ctxn = sb("ctxn", [P, 2, T, D])
        ctxt = sb("ctxt", [P, T * P])
        st3 = sb("st3", [P, 2, T, 6])
        sm3 = sb("sm3", [P, 10, T])
        co3 = sb("co3", [P, 2, 4, T])
        row = sb("row", [P, 4, T, ROWW])
        xg = sb("xg", [P, 2, T, D])
        xgt = sb("xgt", [P, T * P])
        rt = sb("rt", [P, 6, T, E])
        r4 = sb("r4", [P, 7, T])
        oh_bf = sb("oh_bf", [P, T, E], BF16)
        base = sb("base", [P, E])
        pos = sb("pos", [P, 4, T], I32)
        te = sb("te", [1, 16, E])
        tei = sb("tei", [1, 2, E], I32)
        tg = x_flat[0:1, 0:2 * NX * E].rearrange("p (a i e) -> p a i e", a=2, e=E)
        tn = sb("tn", [1, 4, NX])
        ti = sb("ti", [1, 2, NX], I32)
        pad = sb("pad", [P, ROWW])
        er = sb("er", [P, 8, ROWW])
        ex = sb("ex", [P, 2, D])
        ext = sb("ext", [P, 2, P])
        hid = x_flat[:, 2048:2048 + 2 * HID].rearrange("p (k h) -> p k h", k=2)
        hidt = x_flat[:, 3072:3072 + 2 * HID].rearrange("p (k c t) -> p k c t", k=2, c=HC)
        eo = sb("eo", [P, 4, D])

        s_cst = sem("s_cst"); s_wtok = sem("s_wtok"); s_watt = sem("s_watt"); s_wexp = sem("s_wexp")
        s_set = sem("s_set")
        s_bias_ps = sem("s_bias_ps")
        x_in = [sem(f"x_in{i}") for i in range(4 * T)]
        a_stats = sem("a_stats"); a_small = sem("a_small"); a_coef = sem("a_coef")
        a_nv = sem("a_nv"); a_np = sem("a_np"); a_na = sem("a_na")
        a_tr = sem("a_tr"); a_ev = sem("a_ev"); a_mm = sem("a_mm"); a_out = sem("a_out")
        b_stats = sem("b_stats"); b_small = sem("b_small"); b_coef = sem("b_coef"); b_xn = sem("b_xn"); b_xtr = sem("b_xtr")
        b_xt = sem("b_xt"); b_cb = sem("b_cb"); b_cbf = sem("b_cbf"); b_cbs = sem("b_cbs"); b_cbtr = sem("b_cbtr")
        b_cbt = sem("b_cbt"); b_cbrow = [sem(f"b_cbrow{i}") for i in range(2)]
        b_q = sem("b_q"); b_qt = sem("b_qt"); b_k = sem("b_k"); b_kt = sem("b_kt")
        b_kmv = sem("b_kmv"); b_kma = sem("b_kma"); b_v = sem("b_v"); b_va = sem("b_va"); b_vv = sem("b_vv")
        b_sc = sem("b_sc"); b_mx = sem("b_mx"); b_sub = sem("b_sub"); b_exp = sem("b_exp"); b_ptr = sem("b_ptr")
        b_pt = sem("b_pt"); b_pv = sem("b_pv"); b_rd = sem("b_rd"); b_cn = sem("b_cn")
        c_tr = sem("c_tr"); c_ct = sem("c_ct"); c_wd = sem("c_wd"); c_res = sem("c_res"); c_stats = sem("c_stats")
        c_small = sem("c_small"); c_xg = sem("c_xg"); c_xtr = sem("c_xtr"); c_xt = sem("c_xt")
        c_gate = sem("c_gate"); c_rt = sem("c_rt"); c_exp = sem("c_exp"); c_pre = sem("c_pre")
        c_scat = [sem(f"c_scat{i}") for i in range(4)]
        s_tab = sem("s_tab"); s_pad = sem("s_pad"); s_padr = sem("s_padr"); s_w1s = sem("s_w1s")
        e_in = [sem(f"e_in{i}") for i in range(8)]
        e_n = sem("e_n"); e_tr = sem("e_tr"); e_xt = sem("e_xt"); e_f1 = sem("e_f1"); e_hid = sem("e_hid")
        e_htr = sem("e_htr"); e_ht = sem("e_ht"); e_f2 = sem("e_f2"); e_o = sem("e_o")
        e_out = [sem(f"e_out{i}") for i in range(4)]

        x_t = x.rearrange("a (s j) e -> (a s) (j e)", j=TOK)
        block = ctx.enter_context(nc.Block())

        def tile(n):
            return tok_out[:, bass.ds(n, 1), :].rearrange("p o d -> p (o d)")

        SMALL1 = 10
        SMALL2 = 10
        SMALL3 = 14
        ROUTE = 16
        S1, S2, S3, S4, S5, S6, S7 = 1, 2, 3, 4, 5, 6, 7

        def groups(eng, body, lag, first, ways):
            def runs_at(u):
                return lambda k: 0 <= u - k < NG
            for u in range(first):
                body(u, u % ways, runs_at(u))
            turns = (NG - first) // ways
            with eng.Fori(0, turns) as turn:
                for c in range(ways):
                    body(turn * ways + (first + c), (first + c) % ways, lambda k: True)
            for u in range(first + ways * turns, NG + lag):
                body(u, u % ways, runs_at(u))

        def stored(i, k):
            return 16 * (i // 4 + 1) if isinstance(i, int) else (i - k) * 4 + 16

        class Step:
            def __init__(self, i, c):
                self.i, self.c = i, c

            def __call__(self, s):
                return not isinstance(self.i, int) or 0 <= self.i - s < NX

            def k(self, s, ways=2):
                return (self.c - s) % ways

        def tiles3(eng, body, lag):
            for i in range(8):
                body(i, Step(i, i))
            turns = (NX - 8) // 8
            with eng.Fori(0, turns) as turn:
                for c in range(8):
                    body(turn * 8 + (8 + c), Step(turn, c))
            for i in range(8 + 8 * turns, NX + lag):
                body(i, Step(i, i % 8))

        @block.sync
        def _(sp):
            sp.dma_start(cst[:, :], cf).then_inc(s_cst, 16)
            sp.dma_start(cint[:, :], ci).then_inc(s_cst, 16)

            def load_x(i, slot, first):
                if not first:
                    sp.wait_ge(a_tr, i * 4 * T + slot - 4 * T + 1)
                sp.dma_start(xs[:, slot, :, :].rearrange("p j e -> p (j e)"),
                             x_t[bass.ds((i * 4 * T + slot) * P, P), :]).then_inc(x_in[slot], 16)

            for slot in range(4 * T):
                load_x(0, slot, True)
            with sp.Fori(1, NT // (4 * T)) as i:
                for slot in range(4 * T):
                    load_x(i, slot, False)
            for e in range(E):
                sp.dma_start(w1_sb[:, e, :], w1[e]).then_inc(s_wexp, 16)
                sp.dma_start(w2_sb[:, e, :, :], w2[e].rearrange("(c p) d -> p c d", p=P)).then_inc(s_wexp, 16)

            def body(u, par, runs):
                if runs(S1):
                    g = u - S1
                    k = (par - S1) % 2
                    need(sp, b_cbt, g + 1)
                    need(sp, b_sc, T * (g - 2) + T)
                    for r in range(6):
                        c, s = r // 2, r % 2
                        sp.dma_start(cbrow[r:r + 1, k, :, :],
                                     cbt[32 * c:32 * c + 32, SEQ * s:SEQ * s + SEQ].rearrange("a (o s) -> a o s", o=1)
                                     ).then_inc(b_cbrow[k], 16)
            groups(sp, body, S6, 8, 4)

            sp.wait_ge(s_padr, 4)
            for i in range(SPARE):
                sp.dma_start(rows[E * REGION + i * P:E * REGION + (i + 1) * P, :], pad[:, :]).then_inc(s_pad, 16)
            sp.wait_ge(s_tab, 20)
            for e in range(E):
                r = sp.value_load(tei[0:1, 0, e:e + 1], min_val=0, max_val=E * REGION - P)
                sp.dma_start(rows[bass.ds(r, P), :], pad[:, :]).then_inc(s_pad, 16)
            sp.wait_ge(s_pad, 16 * (SPARE + E))
            for k in range(4):
                sp.wait_ge(c_scat[k], 16 * T * NG // 4)

            def load_rows(i, on):
                if not on(0):
                    return
                r = sp.value_load(ti[0:1, 0, bass.ds(i, 1)], min_val=0, max_val=E * REGION + SPARE * P - P)
                if not (isinstance(i, int) and i < 8):
                    sp.wait_ge(e_o, i - 7)
                    sp.wait_ge(e_out[on.k(0, 4)], stored(i - 8, on.k(0, 4)))
                sp.dma_start(er[:, on.k(0, 8), :], rows[bass.ds(r, P), :]).then_inc(e_in[on.k(0, 8)], 16)
            tiles3(sp, load_rows, 0)

        @block.gpsimd
        def _(pool):
            def after(sem_, value):
                if not isinstance(value, int):
                    pool.wait_ge(sem_, value)
                    pool.nop(nofuse=True)
                elif value > 0:
                    pool.wait_ge(sem_, value)

            after(s_cst, 32)
            nc.gpsimd.memset(pad[:, :], 0.0).then_inc(s_padr, 1)
            after(s_padr, 1)
            nc.gpsimd.tensor_copy(pad[:, TOKEN:TOKEN + 1].bitcast(I32), cint[:, NT:NT + 1]).then_inc(s_padr, 1)
            nc.gpsimd.memset(cbrow[:, 0, :, :], 0.0).then_inc(s_padr, 1)
            nc.gpsimd.memset(cbrow[:, 1, :, :], 0.0).then_inc(s_padr, 1)

            def variance(st, sm, n, sem_, v0):
                me, m2e, mo, m2o = (st[:, :, i] for i in (1, 2, 4, 5))
                pool_ = nc.gpsimd
                pool_.tensor_tensor(sm[:, 0, :], me, mo, ALU.subtract).then_inc(sem_, 1)
                pool_.tensor_tensor(sm[:, 1, :], m2e, m2o, ALU.add).then_inc(sem_, 1)
                pool_.tensor_tensor(sm[:, 4, :], me, mo, ALU.add).then_inc(sem_, 1)
                after(sem_, v0 + 3)
                pool_.tensor_tensor(sm[:, 2, :], sm[:, 0, :], sm[:, 0, :], ALU.mult).then_inc(sem_, 1)
                pool_.tensor_scalar(sm[:, 3, :], sm[:, 1, :], 1.0 / D, 0.0, ALU.mult, ALU.add).then_inc(sem_, 1)
                after(sem_, v0 + 5)
                pool_.tensor_scalar(sm[:, 5, :], sm[:, 2, :], 0.25, 0.0, ALU.mult, ALU.add).then_inc(sem_, 1)
                after(sem_, v0 + 6)
                pool_.tensor_tensor(sm[:, 6, :], sm[:, 5, :], sm[:, 3, :], ALU.add).then_inc(sem_, 1)
                after(sem_, v0 + 7)

            def rstd(st, sm, n, eps, rs, nm, sem_, v0):
                pool_ = nc.gpsimd
                variance(st, sm, n, sem_, v0)
                pool_.tensor_scalar(sm[:, 7, :], sm[:, 6, :], 1.0, eps, ALU.mult, ALU.add).then_inc(sem_, 1)
                pool_.tensor_scalar(sm[:, 8, :], sm[:, 4, :], -0.5, 1.0, ALU.mult, ALU.mult).then_inc(sem_, 1)
                after(sem_, v0 + 9)
                pool_.tensor_tensor(rs, sm[:, 7, :], neg_half[:, 0:n], ALU.pow).then_inc(sem_, 1)
                after(sem_, v0 + 10)
                return pool_.tensor_tensor(nm, sm[:, 8, :], rs, ALU.mult)

            def body1(u, par, runs):
                if runs(1):
                    g, k = u - 1, (par - 1) % 2
                    after(a_stats, g + 1)
                    after(a_nv, T * (g - 1))
                    after(a_na, T * (g - 1))
                    rstd(st1[:, k], sm1, T * TOK, EPS_TOK, rs1[:, k, :], nm1[:, k, :], a_small, g * SMALL1
                         ).then_inc(a_coef, 1)
            groups(pool, body1, 1, 4, 4)

            def body2(u, par, runs):
                if runs(S1):
                    g = u - S1
                    v = 4 * g
                    after(b_cbf, g + 1)
                    after(b_cbtr, g)
                    nc.gpsimd.tensor_copy(cb3[:, 0, :], cbf[:, :]).then_inc(b_cbs, 1)
                    after(b_cbs, v + 1)
                    nc.gpsimd.tensor_tensor(cbr[:, :], cbf[:, :], cb3[:, 0, :], ALU.subtract).then_inc(b_cbs, 1)
                    after(b_cbs, v + 2)
                    nc.gpsimd.tensor_copy(cb3[:, 1, :], cbr[:, :]).then_inc(b_cbs, 1)
                    after(b_cbs, v + 3)
                    nc.gpsimd.tensor_tensor(cb3[:, 2, :], cbr[:, :], cb3[:, 1, :], ALU.subtract).then_inc(b_cbs, 1)
                if runs(0):
                    g, k = u, par % 2
                    after(b_stats, g + 1)
                    after(b_xn, g - 1)
                    rstd(st2[:, k], sm2, T, EPS, rs2[:, k, :], nm2[:, k, :], b_small, g * SMALL2).then_inc(b_coef, 1)
                if runs(S7):
                    g, k = u - S7, (par - S7) % 4
                    after(c_rt, ROUTE * (g + 1))
                    after(c_small, SMALL3 * (g + 1))
                    for t in range(T):
                        nc.gpsimd.indirect_dma_start(
                            out=rows[:, :], out_offset=bass.IndirectOffsetOnAxis(ap=pos[:, k, t:t + 1], axis=0),
                            in_=row[:, k, t, :], in_offset=None).then_inc(c_scat[k], 16)
                if runs(S4):
                    g, k, kr = u - S4, (par - S4) % 2, (par - S4) % 4
                    v = SMALL3 * g
                    p_ = nc.gpsimd
                    after(c_stats, g + 1)
                    after(c_xg, g - 1)
                    variance(st3[:, k], sm3, T, c_small, v)
                    p_.tensor_scalar(sm3[:, 7, :], sm3[:, 6, :], 1.0, EPS, ALU.mult, ALU.add).then_inc(c_small, 1)
                    p_.tensor_scalar(sm3[:, 8, :], sm3[:, 6, :], 1.0 + EPS, EPS * EPS, ALU.mult, ALU.add
                                     ).then_inc(c_small, 1)
                    p_.tensor_scalar(sm3[:, 9, :], sm3[:, 4, :], -0.5, 1.0, ALU.mult, ALU.mult).then_inc(c_small, 1)
                    after(c_small, v + 10)
                    p_.tensor_tensor(co3[:, k, 0:2, :], sm3[:, 7:9, :], neg_half[:, 0:2 * T].rearrange("p (a t) -> p a t", a=2),
                                     ALU.pow).then_inc(c_small, 1)
                    after(c_small, v + 11)
                    p_.tensor_tensor(co3[:, k, 2:4, :], co3[:, k, 0:2, :], sm3[:, 9:10, :].to_broadcast([P, 2, T]),
                                     ALU.mult).then_inc(c_small, 1)
                    after(c_small, v + 12)
                    p_.tensor_copy(row[:, kr, :, SCALE:SHIFT + 1].rearrange("p t a -> p a t"), co3[:, k, 1:4:2, :]
                                   ).then_inc(c_small, 1)
                    p_.tensor_copy(row[:, kr, :, TOKEN].bitcast(I32), cint[:, bass.ds(g * T, T)]).then_inc(c_small, 1)
            groups(pool, body2, S7, 8, 4)

            def store(i, on):
                if not on(0):
                    return
                after(e_o, i + 1)
                token = er[:, on.k(0, 8), TOKEN:TOKEN + 1].bitcast(I32)
                nc.gpsimd.indirect_dma_start(
                    out=out, out_offset=bass.IndirectOffsetOnAxis(ap=token, axis=0), in_=eo[:, on.k(0, 4), :],
                    in_offset=None, bounds_check=N - 1, oob_is_err=False).then_inc(e_out[on.k(0, 4)], 16)
            tiles3(pool, store, 0)
            for k in range(4):
                pool.wait_ge(e_out[k], 16 * ((NX + 3 - k) // 4))

        @block.scalar
        def _(act):
            act.dma_start(w_raw[:, :, :], w_tok.rearrange("(j e) o -> e j o", j=TOK)).then_inc(s_wtok, 16)
            act.dma_start(cols[:, 0:1], g_tok).then_inc(s_wtok, 16)
            act.dma_start(cols[:, 1:2], b_tok).then_inc(s_wtok, 16)
            act.dma_start(cols[:, 2:3], g_ffn).then_inc(s_wtok, 16)
            act.dma_start(bias_row[:, 0, :], bias_tok).then_inc(s_wtok, 16)
            act.dma_start(bias_row[:, 1, :], bd).then_inc(s_wtok, 16)
            for i, w in enumerate((wq_t, wk_t, wv_t, wd_t)):
                act.dma_start(wqkvd[:, i, :], w).then_inc(s_watt, 16)
            act.dma_start(wb_sb[:, :], wb_t).then_inc(s_watt, 16)
            act.dma_start(mix_sb[:, :], mix_t).then_inc(s_watt, 16)
            act.dma_start(wg_sb[:, :], w_gate).then_inc(s_watt, 16)

            def evac1(n, k):
                need(act, a_tr, n + 1)
                need(act, a_mm, n - 1)
                nc.scalar.activation(xt[:, k, :], bank[k][:, :], ACT.Copy).then_inc(a_ev, 1)

            def gelu1(g, k):
                need(act, a_mm, T * g + T)
                dst = tok_out[:, bass.ds(g * T, T), :]
                nc.scalar.activation(dst, bank[2 + k][:, :].rearrange("p (t d) -> p t d", t=T), ACT.Gelu).then_inc(a_out, 1)

            def body1(u, par, runs):
                g, k = u - 2, (par - 2) % 2
                if runs(2):
                    need(act, a_coef, g + 1)
                for t in range(T):
                    if runs(2):
                        slot = (par - 2) % 4 * T + t
                        for j in (2, 3):
                            c = t * TOK + j
                            ins = nc.scalar.activation(xs[:, slot, j, :], xs[:, slot, j, :], ACT.Identity,
                                                       bias=nm1[:, k, c:c + 1], scale=rs1[:, k, c:c + 1])
                        ins.then_inc(a_na, 1)
                    if (t > 0 and runs(2)) or (t == 0 and runs(3)):
                        evac1(g * T + t - 1, (t - 1) % 2)
                    if t == 1 and runs(3):
                        gelu1(g - 1, 1 - k)
            groups(act, body1, 3, 4, 4)

            def body2(u, par, runs):
                k1 = (par - S1) % 2
                for t in range(T):
                    s, tt = (S2, t - 1) if t else (S3, T - 1)
                    if runs(s):
                        n = (u - s) * T + tt
                        need(act, b_ptr, n + 1)
                        need(act, b_pv, n - 1)
                        nc.scalar.activation(pt[:, tt % 2, :, :].rearrange("p a b -> p (a b)"), bank[6 + tt % 2][:, :],
                                             ACT.Copy).then_inc(b_pt, 1)
                    g = u - S1
                    if t == 0 and runs(S1):
                        need(act, b_cb, g + 1)
                        need(act, b_cbs, 4 * g)
                        nc.scalar.activation(cbf[:, :], bank[2][:, 0:T * H], ACT.Copy).then_inc(b_cbf, 1)
                        need(act, b_q, g + 1)
                        need(act, b_sc, T * (g - 1))
                        nc.scalar.activation(qt[:, k1, :], bank[3][:, :], ACT.Copy).then_inc(b_qt, 1)
                        need(act, b_k, g + 1)
                        need(act, b_kmv, g - 1)
                        nc.scalar.activation(kt[:, k1, :], bank[2][:, :], ACT.Copy).then_inc(b_kt, 1)
                    if t == 0 and runs(S6):
                        need(act, c_rt, ROUTE * (u - S6) + 2)
                        nc.scalar.activation(rt[:, 1, :, :], rt[:, 0, :, :], ACT.Exp).then_inc(c_exp, 1)
                    if t == 0 and runs(S5):
                        g5, k5 = u - S5, (par - S5) % 2
                        need(act, c_small, SMALL3 * g5 + 12)
                        need(act, c_xtr, g5 - 1)
                        for i in range(T):
                            ins = nc.scalar.activation(xg[:, k5, i, :], row[:, (par - S5) % 4, i, 0:D], ACT.Identity,
                                                       bias=co3[:, k5, 2, i:i + 1], scale=co3[:, k5, 0, i:i + 1])
                        ins.then_inc(c_xg, 1)
                    if t == 1 and runs(S1):
                        need(act, b_v, 2 * g + 1)
                        need(act, b_pv, T * (g - 1))
                        src = bank[3][:, :].rearrange("p (b h d) -> p b h d", b=T, h=HP)
                        nc.scalar.activation(vb[0:64, k1, 0:T, :, 0:DH], src[0:64, :, :, 0:DH], ACT.Copy)
                        nc.scalar.activation(vb[64:128, k1, 0:T, :, VW:VW + DH], src[64:128, :, :, DH:2 * DH],
                                             ACT.Copy).then_inc(b_va, 1)
                        act.wait_ge(b_kt, g + 1)
                    if t in (1, 2, 3) and runs(S1):
                        h = 4 + t
                        ins = nc.scalar.activation(kmix[:, k1, h, :], kt[:, k1, :], ACT.Copy, scale=mix_sb[:, h:h + 1])
                        if t == 3:
                            ins.then_inc(b_kma, 1)
                    if t == 2 and runs(S1):
                        need(act, b_cbtr, g + 1)
                        if runs(S2):
                            kk = (par - S2) % 2
                            gg = u - S2
                            if isinstance(gg, int):
                                act.wait_ge(b_cbrow[kk], 96 * (gg // 2 + 1))
                            else:
                                act.wait_ge(b_cbrow[kk], (gg - kk) * 48 + 96)
                        nc.scalar.activation(cbt[:, :], bank[2][0:96, 0:64].bitcast(BF16), ACT.Copy).then_inc(b_cbt, 1)
                    if t == 2 and runs(0):
                        need(act, b_coef, u + 1)
                        need(act, b_xtr, u - 1)
                        for i in range(T):
                            ins = nc.scalar.activation(xn[:, par % 2, i, :], tile(u * T + i), ACT.Identity,
                                                       bias=nm2[:, par % 2, i:i + 1], scale=rs2[:, par % 2, i:i + 1])
                        ins.then_inc(b_xn, 1)
                    if t == 2 and runs(S5):
                        g5 = u - S5
                        need(act, c_xtr, g5 + 1)
                        need(act, c_gate, g5)
                        nc.scalar.activation(xgt[:, :], bank[3][:, :], ACT.Copy).then_inc(c_xt, 1)
                    if t == 3 and runs(S3):
                        g3 = u - S3
                        need(act, c_tr, g3 + 1)
                        need(act, c_wd, g3)
                        nc.scalar.activation(ctxt[:, :], bank[2][:, :], ACT.Copy).then_inc(c_ct, 1)
                    if runs(S2):
                        n = (u - S2) * T + t
                        need(act, b_sub, n + 1)
                        need(act, b_ptr, n - 1)
                        nc.scalar.activation(pe_[:, t % 2, :], pr[:, t % 2, :, :].rearrange("p h s -> p (h s)"), ACT.Exp,
                                             scale=1.0 / float(D / H) ** 0.5).then_inc(b_exp, 1)
                    if t == 3 and runs(0):
                        need(act, b_xtr, u + 1)
                        need(act, b_v, 2 * (u - 1))
                        nc.scalar.activation(xnt[:, par % 2, :], bank[3][:, :], ACT.Copy).then_inc(b_xt, 1)
            act.wait_ge(s_watt, 16 * 7)
            groups(act, body2, S6, 8, 4)

            act.wait_ge(s_wexp, 32 * E)
            act.wait_ge(s_wtok, 16 * 6)
            def body3(i, on):
                if on(0):
                    need(act, e_tr, i + 1)
                    need(act, e_f1, i - 1)
                    nc.scalar.activation(ext[:, on.k(0), :], bank[0 + on.k(0)][:, 0:P], ACT.Copy).then_inc(e_xt, 1)
                if on(1):
                    need(act, e_f1, i)
                    need(act, e_htr, i - 2)
                    nc.scalar.activation(hid[:, on.k(1), :], bank[2 + on.k(1)][:, :], ACT.Gelu).then_inc(e_hid, 1)
            tiles3(act, body3, 3)

        @block.tensor
        def _(pe):
            mm = nc.tensor.matmul
            pe.wait_ge(s_set, 2)
            pe.wait_ge(s_wtok, 16 * 6)
            for j in range(TOK):
                mm(bank[0][:, 0:D], beta_bc[:, :], w_raw[:, j, :], start=(j == 0), stop=False)
            mm(bank[0][:, 0:D], cst[0:1, C_ONE:C_ONE + P], bias_row[:, 0, :], start=False, stop=True)
            mm(bank[1][:, 0:D], cst[0:1, C_ONE:C_ONE + P], bias_row[:, 1, :], start=True, stop=True).then_inc(s_bias_ps, 1)
            pe.wait_ge(s_set, 20)

            def bias(dst, i, last):
                mm(dst, sel_bf[:, :], bias3[:, i:i + 1, :].to_broadcast([P, T, D]), start=True, stop=last,
                   skip_group_check=True)

            def product1(g, t, k):
                n = g * T + t
                need(pe, a_ev, n + 1)
                if t == 0:
                    need(pe, a_out, g - 1)
                    bias(bank[2 + k][:, :].rearrange("p (t d) -> p t d", t=T), 0, False)
                for j in range(TOK):
                    ins = mm(bank[2 + k][:, t * D:(t + 1) * D], xt[:, t % 2, j * P:(j + 1) * P], w_sc[:, j, :],
                             start=False, stop=(j == TOK - 1 and t == T - 1), skip_group_check=True)
                ins.then_inc(a_mm, 1)

            def body1(u, par, runs):
                g, k = u - 2, (par - 2) % 2
                for t in range(T):
                    if runs(2):
                        n = g * T + t
                        need(pe, a_nv, n + 1)
                        need(pe, a_na, n + 1)
                        need(pe, a_ev, n - 1)
                        for j in range(TOK):
                            ins = nc.tensor.transpose(bank[t % 2][:, j * P:(j + 1) * P],
                                                      xs[:, (par - 2) % 4 * T + t, j, :], ident)
                        ins.then_inc(a_tr, 1)
                    if t > 0 and runs(2):
                        product1(g, t - 1, k)
                    if t == 0 and runs(3):
                        product1(g - 1, T - 1, 1 - k)
            groups(pe, body1, 3, 4, 4)

            pe.wait_ge(a_out, NG)
            pe.wait_ge(s_watt, 16 * 7)
            pe.wait_ge(s_padr, 4)
            wq, wk, wv, wd = (wqkvd[:, i, :] for i in range(4))

            def body2(u, par, runs):
                g0, k0 = u, par % 2
                g1, k1 = u - S1, (par - S1) % 2
                g3, k3 = u - S3, (par - S3) % 2
                g4, k4 = u - S4, (par - S4) % 2
                g5, k5 = u - S5, (par - S5) % 2
                g6 = u - S6

                for t in range(T):
                    if runs(S2):
                        g, k = u - S2, (par - S2) % 2
                        n = g * T + t
                        if t == 0:
                            need(pe, b_kmv, g + 1)
                            need(pe, b_kma, g + 1)
                            if isinstance(g, int):
                                pe.wait_ge(b_cbrow[k], 96 * (g // 2 + 1))
                            else:
                                pe.wait_ge(b_cbrow[k], (g - k) * 48 + 96)
                        need(pe, b_sub, n - 1)
                        sc = bank[4 + t % 2]
                        for s in range(2):
                            c = t * P + s * SEQ
                            mm(sc[s * SEQ:(s + 1) * SEQ, :], qt[:, k, c:c + SEQ], kmix[:, k, :, c:c + SEQ],
                               start=True, stop=False, skip_group_check=True)
                        mm(sc[:, :], ind_bf[:, :], cbrow[:, k, t * H:(t + 1) * H, :], start=False, stop=True,
                           skip_group_check=True).then_inc(b_sc, 1)
                    s, tt = (S2, t - 1) if t else (S3, T - 1)
                    if runs(s):
                        n = (u - s) * T + tt
                        need(pe, b_exp, n + 1)
                        need(pe, b_pt, n - 1)
                        for hp in range(HP):
                            ins = nc.tensor.transpose(bank[6 + tt % 2][:, hp * P:(hp + 1) * P],
                                                      pe_[:, tt % 2, hp * P:(hp + 1) * P], ident)
                        ins.then_inc(b_ptr, 1)
                    s, tt = (S2, t - 2) if t > 1 else (S3, t + 2)
                    n = (u - s) * T + tt
                    if (t == 2 and runs(S6)) or (t == 3 and runs(S5)):
                        if runs(s):
                            need(pe, b_cn, n - 1)
                        else:
                            need(pe, b_cn, T * NG)
                            need(pe, c_rt, ROUTE * (g6 - 1) + 11 if t == 2 else ROUTE * (g5 - 1) + 2)
                    if t == 2 and runs(S6):
                        need(pe, c_rt, ROUTE * g6 + 5)
                        o = oh_bf[:, :, :].rearrange("p t e -> p (t e)")
                        c = PV_END
                        mm(bank[0][:, c:c + T * E], tri_bf[:, :], o, start=True, stop=False, skip_group_check=True)
                        for i in range(T):
                            ins = mm(bank[0][:, c + (i + 1) * E:c + (T + 1) * E], ones_bf[:, :], o[:, 0:(T - i) * E],
                                     start=False, stop=(i == T - 1), skip_group_check=True)
                        ins.then_inc(c_pre, 1)
                    if t == 3 and runs(S5):
                        need(pe, c_xt, g5 + 1)
                        c = PV_END
                        for i in range(T):
                            ins = mm(bank[1][:, c + i * E:c + (i + 1) * E], xgt[:, i * P:(i + 1) * P], wg_sb[:, :],
                                     start=True, stop=True, skip_group_check=True)
                        ins.then_inc(c_gate, 1)
                    if runs(s):
                        g, k = u - s, (par - s) % 2
                        need(pe, b_pt, n + 1)
                        if tt == 0:
                            need(pe, b_va, g + 1)
                            need(pe, b_vv, g + 1)
                        need(pe, b_cn, n - 1)
                        for hp in range(HP):
                            for q in range(2):
                                ins = mm(bank[tt % 2][q * SEQ:(q + 1) * SEQ, hp * 2 * VW:(hp + 1) * 2 * VW],
                                         pt[:, tt % 2, hp, q * SEQ:(q + 1) * SEQ], vb[:, k, 2 * tt + q, hp, :],
                                         start=True, stop=True, skip_group_check=True)
                        ins.then_inc(b_pv, 1)

                    if t == 0 and runs(S1):
                        need(pe, b_xt, g1 + 1)
                        if runs(S4):
                            need(pe, c_ct, g4 + 1)
                        else:
                            need(pe, b_cbt, g1)
                        for i in range(T):
                            ins = mm(bank[2][:, i * H:(i + 1) * H], xnt[:, k1, i * P:(i + 1) * P], wb_sb[:, :],
                                     start=True, stop=True, skip_group_check=True)
                        ins.then_inc(b_cb, 1)
                        mm(bank[3][:, :], wq, xnt[:, k1, :], start=True, stop=True).then_inc(b_q, 1)
                        need(pe, b_cbf, g1 + 1)
                        mm(bank[2][:, :], wk, xnt[:, k1, :], start=True, stop=True).then_inc(b_k, 1)
                    if t == 1 and runs(S1):
                        for i in range(2):
                            need(pe, b_kt if i else b_qt, g1 + 1)
                            for b in range(T):
                                c = (i * T + b) * SEQ
                                for half in range(2):
                                    ins = mm(bank[3 - i][half * 64:(half + 1) * 64, b * D:(b + 1) * D],
                                             xnt[:, k1, c:c + SEQ], wv, start=True, stop=True, skip_group_check=True)
                            ins.then_inc(b_v, 1)
                    if t == 1 and runs(S4):
                        need(pe, c_ct, g4 + 1)
                        if runs(S1):
                            need(pe, b_va, g1 + 1)
                        else:
                            need(pe, c_xt, g5)
                        bias(bank[3][:, :].rearrange("p (t d) -> p t d", t=T), 1, False)
                        for i in range(T):
                            ins = mm(bank[3][:, i * D:(i + 1) * D], ctxt[:, i * P:(i + 1) * P], wd, start=False,
                                     stop=(i == T - 1), skip_group_check=True)
                        ins.then_inc(c_wd, 1)
                    if t == 2 and runs(S1):
                        need(pe, b_cbs, 4 * g1 + 4)
                        need(pe, b_vv, g1 + 1)
                        nc.tensor.transpose(bank[2][0:96, 0:64].bitcast(BF16), cb3[:, :, :].rearrange("p a b -> p (a b)"),
                                            ident_bf[:, :]).then_inc(b_cbtr, 1)
                    if t == 2 and runs(S5):
                        need(pe, c_xg, g5 + 1)
                        if runs(S4):
                            need(pe, c_res, g4 + 1)
                        else:
                            need(pe, c_res, NG)
                            need(pe, c_xt, g5)
                        for i in range(T):
                            ins = nc.tensor.transpose(bank[3][:, i * P:(i + 1) * P], xg[:, k5, i, :], ident)
                        ins.then_inc(c_xtr, 1)
                    if t == 3 and runs(S3):
                        need(pe, b_cn, T * g3 + T)
                        if runs(S1):
                            need(pe, b_cbt, g1 + 1)
                        else:
                            need(pe, b_cbt, NG)
                            need(pe, c_ct, g3)
                        for i in range(T):
                            ins = nc.tensor.transpose(bank[2][:, i * P:(i + 1) * P], ctxn[:, k3, i, :], ident)
                        ins.then_inc(c_tr, 1)
                    if t == 3 and runs(0):
                        need(pe, b_xn, g0 + 1)
                        if runs(S5):
                            need(pe, c_xt, g5 + 1)
                        elif runs(S4):
                            need(pe, c_res, g4 + 1)
                        elif runs(S1):
                            need(pe, b_va, g1 + 1)
                        for i in range(T):
                            ins = nc.tensor.transpose(bank[3][:, i * P:(i + 1) * P], xn[:, k0, i, :], ident)
                        ins.then_inc(b_xtr, 1)
            groups(pe, body2, S6, 8, 4)

            pe.wait_ge(s_w1s, E)
            pe.wait_ge(s_wexp, 32 * E)
            pe.wait_ge(s_tab, 20)
            pe.wait_ge(c_rt, ROUTE * NG)

            def body3(i, on):
                if on(0):
                    need(pe, e_n, i + 1)
                    need(pe, e_xt, i - 1)
                    nc.tensor.transpose(bank[on.k(0)][:, 0:P], ex[:, on.k(0), :], ident).then_inc(e_tr, 1)
                if on(1):
                    e = pe.value_load(ti[0:1, 1, bass.ds(i - 1, 1)], min_val=0, max_val=E - 1)
                    need(pe, e_xt, i)
                    need(pe, e_hid, i - 2)
                    mm(bank[2 + on.k(1)][:, :], ext[:, on.k(1), :], w1_sb[:, bass.ds(e, 1), :], start=True, stop=True
                       ).then_inc(e_f1, 1)
                if on(2):
                    need(pe, e_hid, i - 1)
                    need(pe, e_ht, i - 3)
                    for c in range(HC):
                        ins = nc.tensor.transpose(bank[4 + on.k(2)][:, c * P:(c + 1) * P],
                                                  hid[:, on.k(2), c * P:(c + 1) * P], ident)
                    ins.then_inc(e_htr, 1)
                if on(3):
                    e = pe.value_load(ti[0:1, 1, bass.ds(i - 3, 1)], min_val=0, max_val=E - 1)
                    need(pe, e_ht, i - 2)
                    need(pe, e_o, i - 4)
                    for c in range(HC):
                        ins = mm(bank[6 + on.k(3)][:, 0:D], hidt[:, on.k(3), c, :], w2_sb[:, bass.ds(e, 1), c, :],
                                 start=(c == 0), stop=(c == HC - 1))
                    ins.then_inc(e_f2, 1)
            tiles3(pe, body3, 3)

        @block.vector
        def _(dve):
            v_ = nc.vector
            def step(ins, n):
                ins.then_inc(s_set, 1)
                dve.wait_ge(s_set, n)
            dve.wait_ge(s_cst, 32)
            dve.wait_ge(s_wtok, 16 * 6)
            step(v_.tensor_scalar(beta_bc[:, :], cst[:, C_ONE:C_ONE + P], cols[:, 1:2], None, ALU.mult), 1)
            step(v_.tensor_copy(ident_bf[:, :], ident), 2)
            step(v_.tensor_copy(tri_bf[:, :], cst[:, C_TRI:C_TRI + P]), 3)
            step(v_.tensor_copy(ones_bf[:, :], cst[:, C_ONE:C_ONE + P]), 4)
            step(v_.tensor_copy(ind_bf[:, :], cst[:, C_IND:C_IND + P]), 5)
            step(v_.tensor_copy(sel_bf[:, :], cst[:, C_SEL:C_SEL + P]), 6)
            step(v_.tensor_scalar(w_sc[:, :, :], w_raw[:, :, :], cols[:, 0:1], None, ALU.mult), 7)
            step(v_.memset(bias3[:, :, :], 0.0), 8)
            dve.wait_ge(s_bias_ps, 1)
            step(v_.tensor_copy(bias_f[:, 0, :], bank[0][:, 0:D]), 9)
            step(v_.tensor_copy(bias_f[:, 1, :], bank[1][:, 0:D]), 10)
            step(v_.tensor_copy(bias_hi[:, :, :], bias_f[:, :, :]), 11)
            step(v_.tensor_tensor(bias_r[:, :, :], bias_f[:, :, :], bias_hi[:, :, :], ALU.subtract), 12)
            step(v_.tensor_copy(bias_mid[:, :, :], bias_r[:, :, :]), 13)
            step(v_.tensor_tensor(bias_lo[:, :, :], bias_r[:, :, :], bias_mid[:, :, :], ALU.subtract), 14)
            step(v_.tensor_copy(bias3[0:32, :, :], bias_hi[0:32, :, :]), 15)
            step(v_.tensor_copy(bias3[32:64, :, :], bias_mid[32:64, :, :]), 16)
            step(v_.tensor_copy(bias3[64:96, :, :], bias_lo[64:96, :, :]), 17)
            step(v_.tensor_copy(base[:, :], cst[:, C_BASE:C_BASE + E]), 18)
            step(v_.memset(vb[:, :, :, :, :], 0.0), 19)
            v_.memset(vb[0:64, :, :, :, DH:DH + 1], 1.0)
            step(v_.memset(vb[64:128, :, :, :, 2 * VW - 1:2 * VW], 1.0), 20)

            def body1(u, par, runs):
                for t in range(T):
                    if runs(0):
                        slot = par * T + t
                        if isinstance(u, int):
                            dve.wait_ge(x_in[slot], 16 * (u // 4 + 1))
                        else:
                            dve.wait_ge(x_in[slot], (u - par) * 4 + 16)
                        if t == 0:
                            need(dve, a_coef, u - 1)
                        for j in range(TOK):
                            ins = v_.bn_stats(st1[:, par % 2, t * TOK + j, :], xs[:, slot, j, :])
                        if t == T - 1:
                            ins.then_inc(a_stats, 1)
                    if runs(2):
                        g, k = u - 2, (par - 2) % 2
                        if t == 0:
                            need(dve, a_coef, g + 1)
                        for j in (0, 1):
                            x_j, c = xs[:, (par - 2) % 4 * T + t, j, :], t * TOK + j
                            ins = v_.tensor_scalar(x_j, x_j, rs1[:, k, c:c + 1], nm1[:, k, c:c + 1], ALU.mult, ALU.add)
                        ins.then_inc(a_nv, 1)
            groups(dve, body1, 2, 4, 4)

            dve.wait_ge(s_watt, 16 * 7)

            iota = cst[:, C_IOTA:C_IOTA + T * E].rearrange("p (t e) -> p t e", t=T)
            gate_ps = bank[1][:, PV_END:PV_END + T * E].rearrange("p (t e) -> p t e", t=T)
            pre_ps = bank[0][:, PV_END:PV_END + T * E].rearrange("p (t e) -> p t e", t=T)
            all_ps = bank[0][:, PV_END + T * E:PV_END + (T + 1) * E]

            def route(g, kr, n):
                bc = lambda a: a.unsqueeze(2).to_broadcast([P, T, E])
                need(dve, c_rt, ROUTE * g + n - 1)
                if n == 1:
                    need(dve, c_gate, g + 1)
                    ins = v_.tensor_reduce(r4[:, 0, :], gate_ps, X, ALU.max)
                if n == 2:
                    ins = v_.tensor_tensor(rt[:, 0], gate_ps, bc(r4[:, 0, :]), ALU.subtract)
                if n == 3:
                    ins = v_.scalar_tensor_tensor(rt[:, 2], rt[:, 0], 0.0, iota, ALU.is_equal, ALU.mult)
                if n == 4:
                    ins = v_.tensor_reduce(r4[:, 1, :], rt[:, 2], X, ALU.min)
                if n == 5:
                    ins = v_.tensor_tensor(oh_bf[:, :, :], iota, bc(r4[:, 1, :]), ALU.is_equal)
                if n == 6:
                    need(dve, c_exp, g + 1)
                    ins = v_.tensor_reduce(r4[:, 2, :], rt[:, 1], X, ALU.add)
                if n == 7:
                    ins = v_.scalar_tensor_tensor(rt[:, 3], oh_bf[:, :, :], 1.0, rt[:, 1], ALU.subtract, ALU.mult)
                if n == 8:
                    ins = v_.tensor_reduce(r4[:, 3, :], rt[:, 3], X, ALU.min)
                if n == 9:
                    ins = v_.scalar_tensor_tensor(r4[:, 4, :], r4[:, 2, :], 1e-9, r4[:, 3, :], ALU.mult, ALU.subtract)
                if n == 10:
                    need(dve, c_pre, g + 1)
                    ins = v_.tensor_tensor(rt[:, 4], pre_ps, base[:, :].unsqueeze(1).to_broadcast([P, T, E]), ALU.add)
                if n == 11:
                    ins = v_.tensor_tensor(base[:, :], all_ps, base[:, :], ALU.add)
                if n == 12:
                    ins = v_.tensor_tensor(rt[:, 5], rt[:, 4], oh_bf[:, :, :], ALU.mult)
                if n == 13:
                    ins = v_.tensor_reduce(r4[:, 5, :], rt[:, 5], X, ALU.add)
                if n == 14:
                    ins = v_.tensor_copy(pos[:, kr, :], r4[:, 5, :])
                if n == 15:
                    ins = v_.tensor_scalar(r4[:, 6, :], r4[:, 4, :], 1.0, None, ALU.add)
                if n == 16:
                    ins = v_.reciprocal(row[:, kr, :, GATE], r4[:, 6, :])
                ins.then_inc(c_rt, 1)

            def sent(g, kr):
                return g // 4 * 16 * T if isinstance(g, int) else (g - kr) * (4 * T)

            def body2(u, par, runs):
                k1 = (par - S1) % 2
                g1 = u - S1

                def routed(*steps):
                    if runs(S6):
                        for n in steps:
                            route(u - S6, (par - S6) % 4, n)

                for t in range(T):
                    if runs(S2):
                        n = (u - S2) * T + t
                        need(dve, b_sc, n + 1)
                        sc = bank[4 + t % 2][:, :].rearrange("p (h s) -> p h s", h=H)
                        v_.tensor_reduce(mx[:, t % 2, :], sc, X, ALU.max).then_inc(b_mx, 1)
                    routed((3, 7, 9, 14)[t])
                    if runs(S2):
                        dve.wait_ge(b_mx, n + 1)
                        need(dve, b_exp, n - 1)
                        v_.tensor_tensor(pr[:, t % 2, :, :], sc, mx[:, t % 2, :].unsqueeze(2).to_broadcast([P, H, SEQ]),
                                         ALU.subtract).then_inc(b_sub, 1)
                    if t == 0:
                        routed(4)
                        if runs(0):
                            need(dve, a_out, u + 1)
                            need(dve, b_coef, u - 1)
                            for i in range(T):
                                ins = v_.bn_stats(st2[:, par % 2, i, :], tile(u * T + i))
                            ins.then_inc(b_stats, 1)
                        routed(5)
                    if t == 1 and runs(S1):
                        need(dve, b_kt, g1 + 1)
                        need(dve, b_v, 2 * g1 + 2)
                        need(dve, b_pv, T * (g1 - 1))
                        src = bank[2][:, :].rearrange("p (b h d) -> p b h d", b=T, h=HP)
                        v_.tensor_copy(vb[0:64, k1, T:2 * T, :, 0:DH], src[0:64, :, :, 0:DH])
                        v_.tensor_copy(vb[64:128, k1, T:2 * T, :, VW:VW + DH], src[64:128, :, :, DH:2 * DH]).then_inc(b_vv, 1)
                    if t == 3:
                        routed(15)
                    if t in (1, 2, 3) and runs(S1):
                        for h in ((0,), (1, 2), (3, 4))[t - 1]:
                            ins = v_.tensor_scalar(kmix[:, k1, h, :], kt[:, k1, :], mix_sb[:, h:h + 1], None, ALU.mult)
                        if t == 3:
                            ins.then_inc(b_kmv, 1)
                    s, tt = (S2, t - 2) if t > 1 else (S3, t + 2)
                    cp = bank[tt % 2][:, 0:PV_END].rearrange("p (a b c) -> p a b c", a=HP, b=2)
                    g, k = u - s, (par - s) % 2
                    n = g * T + tt
                    if runs(s):
                        need(dve, b_pv, n + 1)
                    if t == 2:
                        routed(10)
                    if t == 3:
                        routed(16)
                        if runs(S5):
                            route(u - S5, (par - S5) % 4, 1)
                    if runs(s):
                        v_.reciprocal(rden[:, tt % 2, :, :], cp[:, :, :, DH]).then_inc(b_rd, 1)
                    if t < 3:
                        routed((6, 8, 11)[t])
                    elif runs(S5):
                        route(u - S5, (par - S5) % 4, 2)
                    if runs(s):
                        dve.wait_ge(b_rd, n + 1)
                        if tt == 0:
                            need(dve, c_tr, g - 1)
                        v_.tensor_tensor(ctxn[:, k, tt, :].rearrange("p (a b c) -> p a b c", a=HP, b=2), cp[:, :, :, 0:DH],
                                         rden[:, tt % 2, :, :].unsqueeze(3).to_broadcast([P, HP, 2, DH]),
                                         ALU.mult).then_inc(b_cn, 1)
                    if t == 2:
                        routed(12)
                    if t == 2 and runs(S4):
                        g, k, kr = u - S4, (par - S4) % 2, (par - S4) % 4
                        need(dve, c_wd, g + 1)
                        need(dve, c_scat[kr], sent(g, kr))
                        v_.tensor_tensor(row[:, kr, :, 0:D], bank[3][:, :].rearrange("p (t d) -> p t d", t=T),
                                         tok_out[:, bass.ds(g * T, T), :], ALU.add).then_inc(c_res, 1)
                        need(dve, c_small, SMALL3 * (g - 2) + 7)
                        dve.wait_ge(c_res, g + 1)
                        for i in range(T):
                            ins = v_.bn_stats(st3[:, k, i, :], row[:, kr, i, 0:D])
                        ins.then_inc(c_stats, 1)
                    if t == 2:
                        routed(13)
            groups(dve, body2, S6, 8, 4)

            dve.wait_ge(s_wexp, 32 * E)

            def tab(ins, n):
                ins.then_inc(s_tab, 1)
                dve.wait_ge(s_tab, n)
            cb_ = cst[0:1, C_BASE:C_BASE + E]
            tab(v_.tensor_copy(tei[:, 0, :], base[0:1, :]), 1)
            tab(v_.scalar_tensor_tensor(te[:, 0, :], base[0:1, :], float(P - 1), cb_, ALU.add, ALU.subtract), 2)
            tab(v_.tensor_copy(tei[:, 1, :], te[:, 0, :]), 3)
            tab(v_.tensor_scalar(tei[:, 1, :], tei[:, 1, :], 7, None, ALU.arith_shift_right), 4)
            tab(v_.tensor_copy(te[:, 1, :], tei[:, 1, :]), 5)
            tab(v_.tensor_copy(te[:, 2, :], te[:, 1, :]), 6)
            for e in range(1, E):
                tab(v_.tensor_tensor(te[:, 2, e:e + 1], te[:, 2, e - 1:e], te[:, 1, e:e + 1], ALU.add), 6 + e)
            tiles_i = cst[0:1, C_TILE:C_END].rearrange("p (i e) -> p i e", e=E)
            tab(v_.tensor_tensor(tg[:, 0], tiles_i, te[:, 2, :].unsqueeze(1).to_broadcast([1, NX, E]), ALU.is_ge), 12)
            tab(v_.tensor_tensor(tg[:, 1], tg[:, 0], te[:, 1, :].unsqueeze(1).to_broadcast([1, NX, E]), ALU.mult), 13)
            tab(v_.tensor_reduce(tn[:, 0, :], tg[:, 0], X, ALU.add), 14)
            tab(v_.tensor_reduce(tn[:, 1, :], tg[:, 1], X, ALU.add), 15)
            tab(v_.tensor_tensor(tn[:, 2, :], tiles_i[:, :, 0], tn[:, 1, :], ALU.subtract), 16)
            tab(v_.tensor_scalar(tn[:, 2, :], tn[:, 2, :], float(P), None, ALU.mult), 17)
            tab(v_.scalar_tensor_tensor(tn[:, 3, :], tn[:, 0, :], float(REGION), tn[:, 2, :], ALU.mult, ALU.add), 18)
            tab(v_.tensor_copy(ti[:, 0, :], tn[:, 3, :]), 19)
            tab(v_.tensor_scalar(ti[:, 1, :], tn[:, 0, :], float(E - 1), None, ALU.min), 20)
            for e in range(E):
                v_.tensor_scalar(w1_sb[:, e, :], w1_sb[:, e, :], cols[:, 2:3], None, ALU.mult).then_inc(s_w1s, 1)

            def body3(i, on):
                if on(0):
                    dve.wait_ge(e_in[on.k(0, 8)], 16 * (i // 8 + 1) if isinstance(i, int) else (i - on.c) * 2 + 16)
                    need(dve, e_tr, i - 1)
                    r = er[:, on.k(0, 8), :]
                    v_.tensor_scalar(ex[:, on.k(0), :], r[:, 0:D], r[:, SCALE:SCALE + 1], r[:, SHIFT:SHIFT + 1],
                                     ALU.mult, ALU.add).then_inc(e_n, 1)
                if on(2):
                    need(dve, e_htr, i - 1)
                    need(dve, e_f2, i - 3)
                    v_.tensor_copy(hidt[:, on.k(2), :, :].rearrange("p c t -> p (c t)"), bank[4 + on.k(2)][:, :]
                                   ).then_inc(e_ht, 1)
                if on(3):
                    need(dve, e_f2, i - 2)
                    if not (isinstance(i, int) and i < 7):
                        need(dve, e_out[on.k(3, 4)], stored(i - 7, on.k(3, 4)))
                    r = er[:, on.k(3, 8), :]
                    v_.scalar_tensor_tensor(eo[:, on.k(3, 4), :], bank[6 + on.k(3)][:, 0:D], r[:, GATE:GATE + 1], r[:, 0:D],
                                            ALU.mult, ALU.add).then_inc(e_o, 1)
            tiles3(dve, body3, 3)


_OUT = (P, SEQ, D)


def kernel(x, L0_tok_ln_gamma, L0_tok_ln_beta, L0_tok_W, L0_tok_b, L0_attn_Wq, L0_attn_Wk, L0_attn_Wv, L0_attn_Wb,
           L0_attn_mixing, L0_attn_Wd, L0_attn_bd, L0_ffn_w_gating, L0_ffn_gamma, L0_ffn_w1, L0_ffn_w2):
    import concourse.bacc as bacc
    from concourse.bass_utils import run_bass_kernel_spmd

    c, i = constants()
    arrays = {
        "x": x, "w_tok": L0_tok_W, "g_tok": np.reshape(L0_tok_ln_gamma, (D, 1)), "b_tok": np.reshape(L0_tok_ln_beta, (D, 1)),
        "bias_tok": np.reshape(L0_tok_b, (1, D)), "wq_t": np.transpose(L0_attn_Wq), "wk_t": np.transpose(L0_attn_Wk),
        "wv_t": np.transpose(L0_attn_Wv), "wb_t": np.transpose(L0_attn_Wb), "mix_t": np.transpose(L0_attn_mixing),
        "wd_t": np.transpose(L0_attn_Wd), "bd": np.reshape(L0_attn_bd, (1, D)), "w_gate": L0_ffn_w_gating,
        "g_ffn": np.reshape(L0_ffn_gamma, (D, 1)), "w1": L0_ffn_w1, "w2": L0_ffn_w2, "cf": c, "ci": i,
    }
    arrays = {f"in_{n}": np.ascontiguousarray(a) for n, a in arrays.items()}
    nc = bacc.Bacc("TRN2", target_bir_lowering=False, num_devices=1)
    args = [nc.dram_tensor(n, a.shape, mybir.dt.from_np(a.dtype), kind="ExternalInput").ap() for n, a in arrays.items()]
    rows = nc.dram_tensor("rows", ((E * REGION + SPARE * P), ROWW), F32).ap()
    out = nc.dram_tensor("out", (N, D), F32, kind="ExternalOutput").ap()
    build(nc, *args, rows, out)
    r = run_bass_kernel_spmd(nc, [arrays], core_ids=[0])
    return np.reshape(r.results[0]["out"], _OUT)
```

```python
from contextlib import ExitStack

import numpy as np

import concourse.bass as bass
from concourse import mybir

F32 = mybir.dt.float32
BF16 = mybir.dt.bfloat16
I32 = mybir.dt.int32
ALU = mybir.AluOpType
ACT = mybir.ActivationFunctionType
X = mybir.AxisListType.X

P = 128
D = 128
TOK = 4
SEQ = 64
H = 8
DH = D // H
HP = H // 2
VW = DH + 1
PV_END = H * VW
VB = D // 2 + H
E = 6
HID = 512
HC = HID // P
N = 8192
NT = N // P
T = 4
NG = NT // T
REGION = N + P
NX = E - 1 + -(-(N - (E - 1)) // P)
SPARE = NX - NT + 1
ROWW = 132
GATE, TOKEN, SCALE, SHIFT = 128, 129, 130, 131
EPS_TOK, EPS = 1e-6, 1e-5

C_ID, C_TRI, C_ONE, C_SEL, C_IOTA, C_BASE, C_HALF, C_HEAD, C_OF, C_TILE = 0, 128, 256, 384, 512, 536, 544, 560, 568, 572
CB = 3 * T * H
C_END = C_TILE + NX * E


def constants():
    c = np.zeros((P, C_END), np.float32)
    p = np.arange(P)
    c[:, C_ID:C_ID + P] = np.eye(P)
    c[:, C_TRI:C_TRI + P] = p[:, None] < p[None, :]
    c[:, C_ONE:C_ONE + P] = 1.0
    c[:, C_HEAD:C_HEAD + H] = p[:, None] % H == np.arange(H)
    c[:, C_OF:C_OF + T] = p[:, None] // H % T == np.arange(T)
    c[0:96:32, C_SEL:C_SEL + P] = 1.0
    c[:, C_IOTA:C_IOTA + T * E] = np.tile(np.arange(E) - 8.0, T)
    c[:, C_BASE:C_BASE + E] = np.arange(E) * REGION
    c[:, C_HALF:C_HALF + 16] = -0.5
    c[:, C_TILE:C_END] = np.repeat(np.arange(NX), E)
    i = np.zeros((P, NT + 1), np.int32)
    i[:, 0:NT] = p[:, None] + P * np.arange(NT)[None, :]
    i[:, NT] = N + p
    return c, i


def need(eng, sem, value):
    if not isinstance(value, int) or value > 0:
        eng.wait_ge(sem, value)


def build(nc, x, w_tok, narrow, biases, w_att, w1, w2, cf, ci, rows, out):
    ctx = ExitStack()
    with ctx:
        def sb(name, shape, dt=F32):
            return ctx.enter_context(nc.sbuf_tensor(name, shape, dt))

        def sem(name):
            return ctx.enter_context(nc.semaphore(name))

        bank = [ctx.enter_context(nc.psum_tensor(f"bank{i}", [P, 512], F32)) for i in range(8)]

        cst = sb("cst", [P, C_END])
        cint = sb("cint", [P, NT + 1], I32)
        ident = cst[:, C_ID:C_ID + P]
        neg_half = cst[:, C_HALF:C_HALF + 16]
        ident_bf = sb("ident_bf", [P, P], BF16)
        tri_bf = sb("tri_bf", [P, P], BF16)
        ones_bf = sb("ones_bf", [P, P], BF16)
        head_bf = sb("head_bf", [CB, H], BF16)
        of_bf = sb("of_bf", [CB, T, SEQ], BF16)
        sel_bf = sb("sel_bf", [P, P], BF16)
        w_raw = sb("w_raw", [P, TOK, D])
        w_sc = sb("w_sc", [P, TOK, D])
        cols = sb("cols", [P, 3 + H + E])
        mix_sb, wg_sb = cols[:, 3:3 + H], cols[:, 3 + H:3 + H + E]
        beta_bc = sb("beta_bc", [P, P])
        bias_row = sb("bias_row", [1, 2, D])
        bias_f = sb("bias_f", [P, 2, D])
        bias_hi = sb("bias_hi", [P, 2, D], BF16)
        bias_r = sb("bias_r", [P, 2, D])
        bias_mid = sb("bias_mid", [P, 2, D], BF16)
        bias_lo = sb("bias_lo", [P, 2, D], BF16)
        bias3 = sb("bias3", [P, 2, D], BF16)
        w_att_sb = sb("w_att_sb", [P, 4 * D + H])
        wq, wk, wd = (w_att_sb[:, i * D:(i + 1) * D] for i in range(3))
        wv_even, wv_odd = w_att_sb[:, 3 * D:3 * D + VB], w_att_sb[:, 3 * D + VB:4 * D + H]
        w1_sb = sb("w1_sb", [P, E, HID])
        w2_sb = sb("w2_sb", [P, E, HC, D])
        tok_out = sb("tok_out", [P, NT, D])
        xs = sb("xs", [P, 4 * T, TOK, D])
        st1 = sb("st1", [P, 2, T * TOK, 6])
        sm1 = sb("sm1", [P, 8, T * TOK])
        rs1 = sb("rs1", [P, 2, T * TOK])
        nm1 = sb("nm1", [P, 2, T * TOK])
        xt = sb("xt", [P, 2, TOK * P])
        x_flat = xs[:, :, :, :].rearrange("p a j e -> p (a j e)")
        st2 = sb("st2", [P, T, 6])
        mv2 = sb("mv2", [P, 2, T, 2])
        sm2 = sb("sm2", [P, 2, 2, T])
        rs2 = sb("rs2", [P, 2, T])
        nm2 = sb("nm2", [P, 2, T])
        xn = sb("xn", [P, 2, T, D])
        xnt = sb("xnt", [P, 2, T * P])
        qt = sb("qt", [P, 2, T * P])
        kt = sb("kt", [P, 2, T * P])
        kmix = x_flat.rearrange("p (k h c) -> p k h c", k=2, h=H)
        vb = sb("vb", [P, 2, 2 * T, HP, 2 * VW])
        cbf = sb("cbf", [SEQ, 2, T, H])
        cbr = sb("cbr", [SEQ, 2, T, H])
        cb3 = sb("cb3", [P, 2, 3, T, H], BF16)
        cbt = sb("cbt", [CB, P], BF16)
        cbm = sb("cbm", [CB, 2, 2, H, SEQ], BF16)
        mx = sb("mx", [P, 2, H])
        pr = sb("pr", [P, 2, H, SEQ])
        pe_ = sb("pe_", [P, 2, H * SEQ])
        pt = sb("pt", [P, 2, HP, P])
        rden = sb("rden", [P, 2, HP, 2])
        ctxn = sb("ctxn", [P, 2, T, D])
        ctxt = sb("ctxt", [P, T * P])
        st3 = sb("st3", [P, T, 6])
        mv3 = sb("mv3", [P, 2, T, 2])
        sm3 = sb("sm3", [P, 3, T])
        co3 = sb("co3", [P, 2, 4, T])
        row = sb("row", [P, 4, T, ROWW])
        xg = sb("xg", [P, 2, T, D])
        xgt = sb("xgt", [P, T * P])
        rt = sb("rt", [P, 6, T, E])
        r4 = sb("r4", [P, 7, T])
        oh_bf = sb("oh_bf", [P, T, E], BF16)
        base = sb("base", [P, E])
        pos = sb("pos", [P, 4, T], I32)
        te = sb("te", [1, 16, E])
        tei = sb("tei", [1, 2, E], I32)
        tg = x_flat[0:1, 0:2 * NX * E].rearrange("p (a i e) -> p a i e", a=2, e=E)
        tn = sb("tn", [1, 4, NX])
        ti = sb("ti", [1, 2, NX], I32)
        pad = sb("pad", [P, ROWW])
        er = sb("er", [P, 8, ROWW])
        ex = sb("ex", [P, 2, D])
        ext = sb("ext", [P, 2, P])
        w1c = x_flat[:, 2048:2048 + 2 * HID].rearrange("p (k h) -> p k h", k=2)
        hidt = x_flat[:, 3072:3072 + 2 * HID].rearrange("p (k c t) -> p k c t", k=2, c=HC)
        eo = sb("eo", [P, 4, D])

        s_cst = sem("s_cst"); s_wtok = sem("s_wtok"); s_watt = sem("s_watt"); s_wexp = sem("s_wexp")
        s_const = sem("s_const")
        s_vb = sem("s_vb")
        s_set = sem("s_set")
        s_bias_ps = sem("s_bias_ps")
        x_in = [sem(f"x_in{i}") for i in range(4 * T)]
        a_stats = sem("a_stats"); a_small = sem("a_small"); a_coef = sem("a_coef")
        a_nv = sem("a_nv"); a_np = sem("a_np"); a_na = sem("a_na")
        a_tr = sem("a_tr"); a_ev = sem("a_ev"); a_mm = sem("a_mm"); a_out = sem("a_out")
        b_st = sem("b_st"); c_st = sem("c_st"); b_stats = sem("b_stats"); b_small = sem("b_small"); b_coef = sem("b_coef"); b_xn = sem("b_xn"); b_xtr = sem("b_xtr"); b_bd = sem("b_bd")
        b_xt = sem("b_xt"); b_cbs = sem("b_cbs"); b_cbtr = sem("b_cbtr")
        b_cbt = sem("b_cbt"); b_cbm = sem("b_cbm")
        b_q = sem("b_q"); b_qt = sem("b_qt"); b_k = sem("b_k"); b_kt = sem("b_kt")
        b_kmv = sem("b_kmv"); b_kma = sem("b_kma"); b_v = sem("b_v"); b_va = sem("b_va"); b_vv = sem("b_vv")
        b_sc = sem("b_sc"); b_mx = sem("b_mx"); b_sub = sem("b_sub"); b_exp = sem("b_exp"); b_ptr = sem("b_ptr")
        b_pt = sem("b_pt"); b_pv = sem("b_pv"); b_rd = sem("b_rd"); b_cn = sem("b_cn")
        c_tr = sem("c_tr"); c_ct = sem("c_ct"); c_wd = sem("c_wd"); c_res = sem("c_res"); c_stats = sem("c_stats")
        c_small = sem("c_small"); c_xg = sem("c_xg"); c_xtr = sem("c_xtr"); c_xt = sem("c_xt")
        c_gate = sem("c_gate"); c_rt = sem("c_rt"); c_exp = sem("c_exp"); c_pre = sem("c_pre")
        c_scat = [sem(f"c_scat{i}") for i in range(4)]
        s_tab = sem("s_tab"); s_pad = sem("s_pad"); s_padr = sem("s_padr")
        e_in = [sem(f"e_in{i}") for i in range(8)]
        e_n = sem("e_n"); e_w1 = sem("e_w1"); e_tr = sem("e_tr"); e_xt = sem("e_xt"); e_f1 = sem("e_f1")
        e_ht = sem("e_ht"); e_f2 = sem("e_f2"); e_o = sem("e_o")
        e_out = [sem(f"e_out{i}") for i in range(4)]

        x_t = x.rearrange("a (s j) e -> (a s) (j e)", j=TOK)
        block = ctx.enter_context(nc.Block())

        def tile(n):
            return tok_out[:, bass.ds(n, 1), :].rearrange("p o d -> p (o d)")

        SMALL1 = 9
        SMALL2 = 3
        SMALL3 = 7
        ROUTE = 16
        TABLES = 20
        SET_UP = 12
        S1, S2, S3, S4, S5, S6, S7 = 1, 2, 3, 4, 5, 6, 7

        def groups(eng, body, lag, first, ways, start=0):
            def runs_at(u):
                return lambda k: 0 <= u - k < NG
            for u in range(start, first):
                body(u, u % ways, runs_at(u))
            turns = (NG - first) // ways
            with eng.Fori(0, turns) as turn:
                for c in range(ways):
                    body(turn * ways + (first + c), (first + c) % ways, lambda k: True)
            for u in range(first + ways * turns, NG + lag):
                body(u, u % ways, runs_at(u))

        def stored(i, k):
            return 16 * (i // 4 + 1) if isinstance(i, int) else (i - k) * 4 + 16

        class Step:
            def __init__(self, i, c):
                self.i, self.c = i, c

            def __call__(self, s):
                return not isinstance(self.i, int) or 0 <= self.i - s < NX

            def k(self, s, ways=2):
                return (self.c - s) % ways

        def tiles3(eng, body, lag):
            for i in range(8):
                body(i, Step(i, i))
            turns = (NX - 8) // 8
            with eng.Fori(0, turns) as turn:
                for c in range(8):
                    body(turn * 8 + (8 + c), Step(turn, c))
            for i in range(8 + 8 * turns, NX + lag):
                body(i, Step(i, i % 8))

        @block.sync
        def _(sp):
            def load_x(i, slot, first):
                if not first:
                    sp.wait_ge(a_tr, i * 4 * T + slot - 4 * T + 1)
                sp.dma_start(xs[:, slot, :, :].rearrange("p j e -> p (j e)"),
                             x_t[bass.ds((i * 4 * T + slot) * P, P), :]).then_inc(x_in[slot], 16)

            for slot in range(T):
                load_x(0, slot, True)
            sp.dma_start(cst[:, :], cf).then_inc(s_cst, 16)
            sp.dma_start(cint[:, :], ci).then_inc(s_cst, 16)
            for slot in range(T, 4 * T):
                load_x(0, slot, True)
            sp.dma_start(w_att_sb[:, :], w_att).then_inc(s_watt, 16)
            with sp.Fori(1, NT // (4 * T)) as i:
                for slot in range(4 * T):
                    load_x(i, slot, False)
            for e in range(E):
                sp.dma_start(w1_sb[:, e, :], w1[e]).then_inc(s_wexp, 16)
                sp.dma_start(w2_sb[:, e, :, :], w2[e].rearrange("(c p) d -> p c d", p=P)).then_inc(s_wexp, 16)

            sp.wait_ge(s_padr, 2)
            for i in range(SPARE):
                sp.dma_start(rows[E * REGION + i * P:E * REGION + (i + 1) * P, :], pad[:, :]).then_inc(s_pad, 16)
            sp.wait_ge(s_tab, 1)
            for e in range(E):
                r = sp.value_load(tei[0:1, 0, e:e + 1], min_val=0, max_val=E * REGION - P)
                sp.dma_start(rows[bass.ds(r, P), :], pad[:, :]).then_inc(s_pad, 16)
            sp.wait_ge(s_pad, 16 * (SPARE + E))
            for k in range(4):
                sp.wait_ge(c_scat[k], 16 * T * NG // 4)
            sp.wait_ge(s_tab, TABLES)

            def load_rows(i, on):
                if not on(0):
                    return
                r = sp.value_load(ti[0:1, 0, bass.ds(i, 1)], min_val=0, max_val=E * REGION + SPARE * P - P)
                if not (isinstance(i, int) and i < 8):
                    sp.wait_ge(e_o, i - 7)
                    sp.wait_ge(e_out[on.k(0, 4)], stored(i - 8, on.k(0, 4)))
                sp.dma_start(er[:, on.k(0, 8), :], rows[bass.ds(r, P), :]).then_inc(e_in[on.k(0, 8)], 16)
            tiles3(sp, load_rows, 0)

        @block.gpsimd
        def _(pool):
            def after(sem_, value):
                if not isinstance(value, int):
                    pool.wait_ge(sem_, value)
                    pool.nop(nofuse=True)
                elif value > 0:
                    pool.wait_ge(sem_, value)

            nc.gpsimd.memset(vb[:, :, :, :, :], 0.0).then_inc(s_vb, 1)
            pool.wait_ge(s_vb, 1)
            nc.gpsimd.memset(vb[0:64, :, :, :, DH:DH + 1], 1.0).then_inc(s_vb, 1)
            nc.gpsimd.memset(vb[64:128, :, :, :, 2 * VW - 1:2 * VW], 1.0).then_inc(s_vb, 1)
            nc.gpsimd.memset(cb3[SEQ:P, :, :, :, :], 0.0).then_inc(s_vb, 1)
            pool.wait_ge(s_vb, 4)
            nc.gpsimd.memset(pad[:, :], 0.0).then_inc(s_padr, 1)
            pool.wait_ge(s_padr, 1)
            pool.wait_ge(s_cst, 32)
            nc.gpsimd.tensor_copy(pad[:, TOKEN:TOKEN + 1].bitcast(I32), cint[:, NT:NT + 1]).then_inc(s_padr, 1)

            def rstd(st, sm, n, eps, rs, nm, sem_, v0):
                me, m2e, mo, m2o = (st[:, :, i] for i in (1, 2, 4, 5))
                pool_ = nc.gpsimd
                pool_.tensor_tensor(sm[:, 0, :], me, mo, ALU.subtract).then_inc(sem_, 1)
                pool_.tensor_tensor(sm[:, 1, :], m2e, m2o, ALU.add).then_inc(sem_, 1)
                pool_.tensor_tensor(sm[:, 4, :], me, mo, ALU.add).then_inc(sem_, 1)
                after(sem_, v0 + 3)
                pool_.tensor_tensor(sm[:, 2, :], sm[:, 0, :], sm[:, 0, :], ALU.mult).then_inc(sem_, 1)
                pool_.tensor_scalar(sm[:, 3, :], sm[:, 1, :], 1.0 / D, eps, ALU.mult, ALU.add).then_inc(sem_, 1)
                pool_.tensor_scalar(sm[:, 7, :], sm[:, 4, :], -0.5, 1.0, ALU.mult, ALU.mult).then_inc(sem_, 1)
                after(sem_, v0 + 6)
                pool_.tensor_scalar(sm[:, 5, :], sm[:, 2, :], 0.25, 0.0, ALU.mult, ALU.add).then_inc(sem_, 1)
                after(sem_, v0 + 7)
                pool_.tensor_tensor(sm[:, 6, :], sm[:, 5, :], sm[:, 3, :], ALU.add).then_inc(sem_, 1)
                after(sem_, v0 + 8)
                pool_.tensor_tensor(rs, sm[:, 6, :], neg_half[:, 0:n], ALU.pow).then_inc(sem_, 1)
                after(sem_, v0 + 9)
                return pool_.tensor_tensor(nm, sm[:, 7, :], rs, ALU.mult)

            def body1(u, par, runs):
                if runs(1):
                    g, k = u - 1, (par - 1) % 2
                    after(a_stats, g + 1)
                    after(a_nv, T * (g - 1))
                    after(a_na, T * (g - 1))
                    rstd(st1[:, k], sm1, T * TOK, EPS_TOK, rs1[:, k, :], nm1[:, k, :], a_small, g * SMALL1
                         ).then_inc(a_coef, 1)
            groups(pool, body1, 1, 4, 4)

            def scatter(g, k, tiles):
                after(c_rt, ROUTE * (g + 1))
                after(c_small, SMALL3 * (g + 1))
                for t in tiles:
                    nc.gpsimd.indirect_dma_start(
                        out=rows[:, :], out_offset=bass.IndirectOffsetOnAxis(ap=pos[:, k, t:t + 1], axis=0),
                        in_=row[:, k, t, :], in_offset=None).then_inc(c_scat[k], 16)

            pool.wait_ge(s_set, SET_UP)
            pool.wait_ge(s_const, 7)
            def body2(u, par, runs):
                ending = isinstance(u, int) and u >= NG
                if runs(0):
                    g, k = u, par % 2
                    after(b_stats, g + 1)
                    after(b_xn, g - 1)
                    v = SMALL2 * g
                    nc.gpsimd.tensor_scalar(sm2[:, k, 0, :], mv2[:, k, :, 1], 1.0, EPS, ALU.mult, ALU.add).then_inc(b_small, 1)
                    nc.gpsimd.tensor_scalar(sm2[:, k, 1, :], mv2[:, k, :, 0], -1.0, 1.0, ALU.mult, ALU.mult).then_inc(b_small, 1)
                    after(b_small, v + 2)
                    nc.gpsimd.tensor_tensor(rs2[:, k, :], sm2[:, k, 0, :], neg_half[:, 0:T], ALU.pow).then_inc(b_small, 1)
                    after(b_small, v + 3)
                    nc.gpsimd.tensor_tensor(nm2[:, k, :], sm2[:, k, 1, :], rs2[:, k, :], ALU.mult).then_inc(b_coef, 1)
                behind = runs(S7) and not (ending and u > NG)
                if behind:
                    scatter(u - S7, (par - S7) % 4, (0, 1))
                if runs(S1):
                    g = u - S1
                    after(b_xn, g + 1)
                    o = tok_out[:, bass.ds(g * T, T), :]
                    nc.gpsimd.tensor_tensor(o, o, bias_f[:, 1:2, :].to_broadcast([P, T, D]), ALU.add).then_inc(b_bd, 1)
                if runs(S1):
                    g = u - S1
                    v = 4 * g
                    after(b_va, g + 1)
                    after(b_vv, g + 1)
                    after(b_cbtr, g)
                    nc.gpsimd.tensor_copy(cb3[0:SEQ, :, 0], cbf[:, :, :, :]).then_inc(b_cbs, 1)
                    after(b_cbs, v + 1)
                    nc.gpsimd.tensor_tensor(cbr[:, :, :, :], cbf[:, :, :, :], cb3[0:SEQ, :, 0], ALU.subtract).then_inc(b_cbs, 1)
                    after(b_cbs, v + 2)
                    nc.gpsimd.tensor_copy(cb3[0:SEQ, :, 1], cbr[:, :, :, :]).then_inc(b_cbs, 1)
                    after(b_cbs, v + 3)
                    nc.gpsimd.tensor_tensor(cb3[0:SEQ, :, 2], cbr[:, :, :, :], cb3[0:SEQ, :, 1], ALU.subtract).then_inc(b_cbs, 1)
                if behind:
                    scatter(u - S7, (par - S7) % 4, (2, 3))
                if runs(S1):
                    g, k = u - S1, (par - S1) % 2
                    after(b_cbt, g + 1)
                    after(b_sc, T * (g - 1))
                    nc.gpsimd.tensor_tensor(
                        cbm[:, k, :, :, :],
                        cbt[:, :].rearrange("p (q s) -> p q s", q=2).unsqueeze(2).to_broadcast([CB, 2, H, SEQ]),
                        head_bf[:, :].unsqueeze(1).unsqueeze(3).to_broadcast([CB, 2, H, SEQ]), ALU.mult
                        ).then_inc(b_cbm, 1)
                if runs(S4):
                    g, k, kr = u - S4, (par - S4) % 2, (par - S4) % 4
                    v = SMALL3 * g
                    p_ = nc.gpsimd
                    after(c_stats, g + 1)
                    after(c_xg, g - 1)
                    mean, var = mv3[:, k, :, 0], mv3[:, k, :, 1]
                    p_.tensor_scalar(sm3[:, 0, :], var, 1.0, EPS, ALU.mult, ALU.add).then_inc(c_small, 1)
                    p_.tensor_scalar(sm3[:, 1, :], var, 1.0 + EPS, EPS * EPS, ALU.mult, ALU.add
                                     ).then_inc(c_small, 1)
                    p_.tensor_scalar(sm3[:, 2, :], mean, -1.0, 1.0, ALU.mult, ALU.mult).then_inc(c_small, 1)
                    after(c_small, v + 3)
                    p_.tensor_tensor(co3[:, k, 0:2, :], sm3[:, 0:2, :], neg_half[:, 0:2 * T].rearrange("p (a t) -> p a t", a=2),
                                     ALU.pow).then_inc(c_small, 1)
                    after(c_small, v + 4)
                    p_.tensor_tensor(co3[:, k, 2:4, :], co3[:, k, 0:2, :], sm3[:, 2:3, :].to_broadcast([P, 2, T]),
                                     ALU.mult).then_inc(c_small, 1)
                    after(c_small, v + 5)
                    p_.tensor_copy(row[:, kr, :, SCALE:SHIFT + 1].rearrange("p t a -> p a t"), co3[:, k, 1:4:2, :]
                                   ).then_inc(c_small, 1)
                    p_.tensor_copy(row[:, kr, :, TOKEN].bitcast(I32), cint[:, bass.ds(g * T, T)]).then_inc(c_small, 1)
                if ending and runs(S6):
                    scatter(u - S6, (par - S6) % 4, (0, 1, 2, 3))
            groups(pool, body2, S6, 8, 4)

            def store(i, on):
                if not on(0):
                    return
                after(e_o, i + 1)
                token = er[:, on.k(0, 8), TOKEN:TOKEN + 1].bitcast(I32)
                nc.gpsimd.indirect_dma_start(
                    out=out, out_offset=bass.IndirectOffsetOnAxis(ap=token, axis=0), in_=eo[:, on.k(0, 4), :],
                    in_offset=None, bounds_check=N - 1, oob_is_err=False).then_inc(e_out[on.k(0, 4)], 16)
            tiles3(pool, store, 0)
            for k in range(4):
                pool.wait_ge(e_out[k], 16 * ((NX + 3 - k) // 4))

        @block.scalar
        def _(act):
            act.dma_start(w_raw[:, :, :], w_tok.rearrange("(j e) o -> e j o", j=TOK)).then_inc(s_wtok, 16)
            act.dma_start(cols[:, :], narrow).then_inc(s_wtok, 16)
            act.dma_start(bias_row[:, :, :].rearrange("a b d -> a (b d)"), biases).then_inc(s_wtok, 16)

            act.wait_ge(s_cst, 32)
            for dst, src in (
                (sel_bf[:, :], cst[:, C_SEL:C_SEL + P]), (ident_bf[:, :], ident), (tri_bf[:, :], cst[:, C_TRI:C_TRI + P]),
                (ones_bf[:, :], cst[:, C_ONE:C_ONE + P]), (head_bf[:, :], cst[0:CB, C_HEAD:C_HEAD + H]),
                (of_bf[:, :, :], cst[0:CB, C_OF:C_OF + T].unsqueeze(2).to_broadcast([CB, T, SEQ])),
                (base[:, :], cst[:, C_BASE:C_BASE + E]),
            ):
                nc.scalar.activation(dst, src, ACT.Copy).then_inc(s_const, 1)

            def evac1(n, k):
                need(act, a_tr, n + 1)
                need(act, a_mm, n - 1)
                nc.scalar.activation(xt[:, k, :], bank[4 + k][:, :], ACT.Copy).then_inc(a_ev, 1)

            def gelu1(g, k):
                need(act, a_mm, T * g + T)
                dst = tok_out[:, bass.ds(g * T, T), :]
                nc.scalar.activation(dst, bank[6 + k][:, :].rearrange("p (t d) -> p t d", t=T), ACT.Gelu).then_inc(a_out, 1)

            def body1(u, par, runs):
                g, k = u - 2, (par - 2) % 2
                if runs(2):
                    need(act, a_coef, g + 1)
                for t in range(T):
                    if runs(2):
                        slot = (par - 2) % 4 * T + t
                        for j in (2, 3):
                            c = t * TOK + j
                            ins = nc.scalar.activation(xs[:, slot, j, :], xs[:, slot, j, :], ACT.Identity,
                                                       bias=nm1[:, k, c:c + 1], scale=rs1[:, k, c:c + 1])
                        ins.then_inc(a_na, 1)
                    if (t > 0 and runs(2)) or (t == 0 and runs(3)):
                        evac1(g * T + t - 1, (t - 1) % 2)
                    if t == 1 and isinstance(u, int) and u == NG + 1:
                        norm(0, 0, (0, 1, 2, 3))
                    if t == 0 and isinstance(u, int) and u == NG + 2:
                        norm_turned(0, 0)
                    if t == 1 and runs(3):
                        gelu1(g - 1, 1 - k)

            def norm(g, k, tiles):
                if 0 in tiles:
                    need(act, b_coef, g + 1)
                    need(act, b_xtr, g - 1)
                for i in tiles:
                    ins = nc.scalar.activation(xn[:, k, i, :], tile(g * T + i), ACT.Identity,
                                               bias=nm2[:, k, i:i + 1], scale=rs2[:, k, i:i + 1])
                if T - 1 in tiles:
                    ins.then_inc(b_xn, 1)

            def norm_turned(g, k):
                need(act, b_xtr, g + 1)
                need(act, b_v, 2 * (g - 1))
                nc.scalar.activation(xnt[:, k, :], bank[3][:, :], ACT.Copy).then_inc(b_xt, 1)
            groups(act, body1, 3, 4, 4)

            def body2(u, par, runs):
                k1 = (par - S1) % 2
                g1, g3, g5, g6 = u - S1, u - S3, u - S5, u - S6

                def norm_routed(tiles):
                    k5 = (par - S5) % 2
                    if 0 in tiles:
                        need(act, c_small, SMALL3 * g5 + 5)
                        need(act, c_xtr, g5 - 1)
                    for i in tiles:
                        ins = nc.scalar.activation(xg[:, k5, i, :], row[:, (par - S5) % 4, i, 0:D], ACT.Identity,
                                                   bias=co3[:, k5, 2, i:i + 1], scale=co3[:, k5, 0, i:i + 1])
                    if T - 1 in tiles:
                        ins.then_inc(c_xg, 1)

                for t in range(T):
                    s, tt = (S2, t - 1) if t else (S3, T - 1)
                    if runs(s):
                        n = (u - s) * T + tt
                        need(act, b_ptr, n + 1)
                        need(act, b_pv, n - 1)
                        nc.scalar.activation(pt[:, tt % 2, :, :].rearrange("p a b -> p (a b)"), bank[6 + tt % 2][:, :],
                                             ACT.Copy).then_inc(b_pt, 1)
                    if t == 0 and runs(S6):
                        need(act, c_rt, ROUTE * g6 + 2)
                        nc.scalar.activation(rt[:, 1, :, :], rt[:, 0, :, :], ACT.Exp).then_inc(c_exp, 1)
                    if t == 1 and runs(S5):
                        norm_routed((2, 3))
                    if t in (2, 3) and runs(0):
                        norm(u, par % 2, (2 * t - 4, 2 * t - 3))
                    if runs(S2):
                        n = (u - S2) * T + t
                        need(act, b_sub, n + 1)
                        need(act, b_ptr, n - 1)
                        nc.scalar.activation(pe_[:, t % 2, :], pr[:, t % 2, :, :].rearrange("p h s -> p (h s)"), ACT.Exp,
                                             scale=1.0 / float(D / H) ** 0.5).then_inc(b_exp, 1)
                    if t == 0 and runs(S1):
                        need(act, b_q, g1 + 1)
                        need(act, b_sc, T * (g1 - 1))
                        nc.scalar.activation(qt[:, k1, :], bank[3][:, :], ACT.Copy).then_inc(b_qt, 1)
                        need(act, b_k, g1 + 1)
                        need(act, b_kmv, g1 - 1)
                        nc.scalar.activation(kt[:, k1, :], bank[2][:, :], ACT.Copy).then_inc(b_kt, 1)
                    if t == 0 and runs(S5):
                        norm_routed((0, 1))
                    if t == 1 and runs(S1):
                        need(act, b_v, 2 * g1 + 2)
                        need(act, b_pv, T * (g1 - 1))
                        need(act, b_cbs, 4 * g1)
                        src = bank[3][:, 0:T * VB].rearrange("p (b w) -> p b w", b=T)
                        v = src[:, :, 0:D // 2].rearrange("p b (h d) -> p b h d", h=HP)
                        nc.scalar.activation(cbf[:, :, 0:2, :].rearrange("p q t h -> p t q h"),
                                             src[0:SEQ, :, D // 2:VB].rearrange("p (t q) h -> p t q h", q=2), ACT.Copy)
                        nc.scalar.activation(vb[0:64, k1, 0:T, :, 0:DH], v[0:64], ACT.Copy)
                        nc.scalar.activation(vb[64:128, k1, 0:T, :, VW:VW + DH], v[64:128], ACT.Copy).then_inc(b_va, 1)
                        act.wait_ge(b_kt, g1 + 1)
                    if t == 2 and runs(S5):
                        need(act, c_xtr, g5 + 1)
                        need(act, c_gate, g5)
                        nc.scalar.activation(xgt[:, :], bank[3][:, :], ACT.Copy).then_inc(c_xt, 1)
                    if t == 2 and runs(S1):
                        need(act, b_cbtr, g1 + 1)
                        need(act, b_cbm, g1)
                        nc.scalar.activation(cbt[:, :].rearrange("p (q s) -> p q s", q=2),
                                             bank[2][0:CB, 0:P].bitcast(BF16).rearrange("p (q s) -> p q s", q=2)[:, :, 0:SEQ],
                                             ACT.Copy).then_inc(b_cbt, 1)
                    if t in (1, 2) and runs(S1):
                        h = 5 + t
                        ins = nc.scalar.activation(kmix[:, k1, h, :], kt[:, k1, :], ACT.Copy, scale=mix_sb[:, h:h + 1])
                        if t == 2:
                            ins.then_inc(b_kma, 1)
                    if t == 3 and runs(S3):
                        need(act, c_tr, g3 + 1)
                        need(act, c_wd, g3)
                        nc.scalar.activation(ctxt[:, :], bank[2][:, :], ACT.Copy).then_inc(c_ct, 1)
                    if t == 3 and runs(0):
                        norm_turned(u, par % 2)
            act.wait_ge(s_watt, 16)
            act.wait_ge(s_vb, 4)
            groups(act, body2, S6, 8, 4, start=1)

            act.wait_ge(c_rt, ROUTE * NG)
            def body3(i, on):
                if on(1):
                    need(act, e_tr, i)
                    need(act, e_f1, i - 2)
                    nc.scalar.activation(ext[:, on.k(1), :], bank[0 + on.k(1)][:, 0:P], ACT.Copy).then_inc(e_xt, 1)
                if on(2):
                    need(act, e_f1, i - 1)
                    need(act, e_f2, i - 3)
                    nc.scalar.activation(hidt[:, on.k(2), :, :].rearrange("p c t -> p (c t)"), bank[2 + on.k(2)][:, :],
                                         ACT.Gelu).then_inc(e_ht, 1)
            tiles3(act, body3, 3)

        @block.tensor
        def _(pe):
            mm = nc.tensor.matmul
            pe.wait_ge(s_set, 1)
            pe.wait_ge(s_cst, 32)
            pe.wait_ge(s_wtok, 16 * 3)
            for j in range(TOK):
                mm(bank[0][:, 0:D], beta_bc[:, :], w_raw[:, j, :], start=(j == 0), stop=False)
            mm(bank[0][:, 0:D], cst[0:1, C_ONE:C_ONE + P], bias_row[:, 0, :], start=False, stop=True)
            mm(bank[1][:, 0:D], cst[0:1, C_ONE:C_ONE + P], bias_row[:, 1, :], start=True, stop=True).then_inc(s_bias_ps, 1)
            pe.wait_ge(s_set, SET_UP)
            pe.wait_ge(s_const, 7)

            def bias(dst, i, last):
                mm(dst, sel_bf[:, :], bias3[:, i:i + 1, :].to_broadcast([P, T, D]), start=True, stop=last,
                   skip_group_check=True)

            def product1(g, t, k):
                n = g * T + t
                need(pe, a_ev, n + 1)
                if t == 0:
                    need(pe, a_out, g - 1)
                    bias(bank[6 + k][:, :].rearrange("p (t d) -> p t d", t=T), 0, False)
                for j in range(TOK):
                    ins = mm(bank[6 + k][:, t * D:(t + 1) * D], xt[:, t % 2, j * P:(j + 1) * P], w_sc[:, j, :],
                             start=False, stop=(j == TOK - 1 and t == T - 1), skip_group_check=True)
                ins.then_inc(a_mm, 1)

            def body1(u, par, runs):
                g, k = u - 2, (par - 2) % 2
                for t in range(T):
                    if runs(2):
                        n = g * T + t
                        need(pe, a_nv, n + 1)
                        need(pe, a_na, n + 1)
                        need(pe, a_ev, n - 1)
                        for j in range(TOK):
                            ins = nc.tensor.transpose(bank[4 + t % 2][:, j * P:(j + 1) * P],
                                                      xs[:, (par - 2) % 4 * T + t, j, :], ident)
                        ins.then_inc(a_tr, 1)
                    if t > 0 and runs(2):
                        product1(g, t - 1, k)
                    if t == 0 and runs(3):
                        product1(g - 1, T - 1, 1 - k)
                if isinstance(u, int) and u == NG + 1:
                    turn_norm(0, 0)

            def turn_norm(g, k):
                need(pe, b_xn, g + 1)
                for i in range(T):
                    ins = nc.tensor.transpose(bank[3][:, i * P:(i + 1) * P], xn[:, k, i, :], ident)
                ins.then_inc(b_xtr, 1)
            groups(pe, body1, 3, 4, 4)

            pe.wait_ge(s_vb, 4)
            pe.wait_ge(s_watt, 16)

            def body2(u, par, runs):
                g0, k0 = u, par % 2
                g1, k1 = u - S1, (par - S1) % 2
                g3, k3 = u - S3, (par - S3) % 2
                g4, k4 = u - S4, (par - S4) % 2
                g5, k5 = u - S5, (par - S5) % 2
                g6 = u - S6

                for t in range(T):
                    if runs(S2):
                        g, k = u - S2, (par - S2) % 2
                        n = g * T + t
                        if isinstance(g, int) and g == 0 and t == 0:
                            pe.wait_ge(a_out, NG)
                        if t == 0:
                            need(pe, b_kmv, g + 1)
                            need(pe, b_kma, g + 1)
                            need(pe, b_cbm, g + 1)
                        need(pe, b_sub, n - 1)
                        sc = bank[4 + t % 2]
                        for s in range(2):
                            c = t * P + s * SEQ
                            mm(sc[s * SEQ:(s + 1) * SEQ, :], qt[:, k, c:c + SEQ], kmix[:, k, :, c:c + SEQ],
                               start=True, stop=False, skip_group_check=True)
                        for s in range(2):
                            ins = mm(sc[s * SEQ:(s + 1) * SEQ, :], of_bf[:, t, :], cbm[:, k, s, :, :], start=False, stop=True,
                                     skip_group_check=True)
                        ins.then_inc(b_sc, 1)
                    if t == 1 and runs(S4):
                        need(pe, c_ct, g4 + 1)
                        if runs(S1):
                            need(pe, b_qt, g1 + 1)
                        else:
                            need(pe, c_xt, g5)
                        for i in range(T):
                            ins = mm(bank[3][:, i * D:(i + 1) * D], ctxt[:, i * P:(i + 1) * P], wd, start=True,
                                     stop=True, skip_group_check=True)
                        ins.then_inc(c_wd, 1)
                    s, tt = (S2, t - 1) if t else (S3, T - 1)
                    if runs(s):
                        n = (u - s) * T + tt
                        need(pe, b_exp, n + 1)
                        need(pe, b_pt, n - 1)
                        for hp in range(HP):
                            ins = nc.tensor.transpose(bank[6 + tt % 2][:, hp * P:(hp + 1) * P],
                                                      pe_[:, tt % 2, hp * P:(hp + 1) * P], ident)
                        ins.then_inc(b_ptr, 1)
                    s, tt = (S2, t - 2) if t > 1 else (S3, t + 2)
                    n = (u - s) * T + tt
                    if (t == 2 and runs(S6)) or (t == 3 and runs(S5)):
                        if runs(s):
                            need(pe, b_cn, n - 1)
                        else:
                            need(pe, b_cn, T * NG)
                            need(pe, c_rt, ROUTE * (g6 - 1) + 11 if t == 2 else ROUTE * (g5 - 1) + 2)
                    if t == 2 and runs(S6):
                        need(pe, c_rt, ROUTE * g6 + 5)
                        o = oh_bf[:, :, :].rearrange("p t e -> p (t e)")
                        c = PV_END
                        mm(bank[0][:, c:c + T * E], tri_bf[:, :], o, start=True, stop=False, skip_group_check=True)
                        for i in range(T):
                            ins = mm(bank[0][:, c + (i + 1) * E:c + (T + 1) * E], ones_bf[:, :], o[:, 0:(T - i) * E],
                                     start=False, stop=(i == T - 1), skip_group_check=True)
                        ins.then_inc(c_pre, 1)
                    if t == 3 and runs(S5):
                        need(pe, c_xt, g5 + 1)
                        c = PV_END
                        for i in range(T):
                            ins = mm(bank[1][:, c + i * E:c + (i + 1) * E], xgt[:, i * P:(i + 1) * P], wg_sb,
                                     start=True, stop=True, skip_group_check=True)
                        ins.then_inc(c_gate, 1)
                    if runs(s):
                        g, k = u - s, (par - s) % 2
                        need(pe, b_pt, n + 1)
                        if tt == 0:
                            need(pe, b_va, g + 1)
                            need(pe, b_vv, g + 1)
                        need(pe, b_cn, n - 1)
                        for hp in range(HP):
                            for q in range(2):
                                ins = mm(bank[tt % 2][q * SEQ:(q + 1) * SEQ, hp * 2 * VW:(hp + 1) * 2 * VW],
                                         pt[:, tt % 2, hp, q * SEQ:(q + 1) * SEQ], vb[:, k, 2 * tt + q, hp, :],
                                         start=True, stop=True, skip_group_check=True)
                        ins.then_inc(b_pv, 1)

                    if t == 0 and runs(S1):
                        need(pe, b_xt, g1 + 1)
                        if runs(S4):
                            need(pe, c_ct, g4 + 1)
                        else:
                            need(pe, b_cbt, g1)
                        mm(bank[3][:, :], wq, xnt[:, k1, :], start=True, stop=True).then_inc(b_q, 1)
                        mm(bank[2][:, :], wk, xnt[:, k1, :], start=True, stop=True).then_inc(b_k, 1)
                    if t == 1 and runs(S1):
                        for i in (1, 0):
                            need(pe, b_kt if i else b_qt, g1 + 1)
                            if i == 0 and runs(S4):
                                need(pe, c_res, g4 + 1)
                            for b in range(T):
                                c = (i * T + b) * SEQ
                                mm(bank[3 - i][0:64, b * VB:b * VB + VB], xnt[:, k1, c:c + SEQ], wv_even,
                                   start=True, stop=True, skip_group_check=True)
                                ins = mm(bank[3 - i][64:128, b * VB:b * VB + D // 2], xnt[:, k1, c:c + SEQ], wv_odd,
                                         start=True, stop=True, skip_group_check=True)
                            ins.then_inc(b_v, 1)
                    if t == 2 and runs(S5):
                        need(pe, c_xg, g5 + 1)
                        if runs(S1):
                            need(pe, b_va, g1 + 1)
                        elif runs(S4):
                            need(pe, c_res, g4 + 1)
                        else:
                            need(pe, c_xt, g5)
                        for i in range(T):
                            ins = nc.tensor.transpose(bank[3][:, i * P:(i + 1) * P], xg[:, k5, i, :], ident)
                        ins.then_inc(c_xtr, 1)
                    if t == 2 and runs(S1):
                        need(pe, b_cbs, 4 * g1 + 4)
                        need(pe, b_vv, g1 + 1)
                        for q in range(2):
                            ins = nc.tensor.transpose(bank[2][0:CB, q * P // 2:(q + 1) * P // 2].bitcast(BF16),
                                                      cb3[:, q].rearrange("p a t h -> p (a t h)"), ident_bf[:, :])
                        ins.then_inc(b_cbtr, 1)
                    if t == 3 and runs(S3):
                        need(pe, b_cn, T * g3 + T)
                        if runs(S1):
                            need(pe, b_cbt, g1 + 1)
                        else:
                            need(pe, b_cbt, NG)
                            need(pe, c_ct, g3)
                        for i in range(T):
                            ins = nc.tensor.transpose(bank[2][:, i * P:(i + 1) * P], ctxn[:, k3, i, :], ident)
                        ins.then_inc(c_tr, 1)
                    if t == 3 and runs(0):
                        if runs(S5):
                            need(pe, c_xt, g5 + 1)
                        elif runs(S4):
                            need(pe, c_res, g4 + 1)
                        elif runs(S1):
                            need(pe, b_va, g1 + 1)
                        turn_norm(g0, k0)
            groups(pe, body2, S6, 8, 4, start=1)

            pe.wait_ge(s_wexp, 32 * E)
            pe.wait_ge(s_tab, TABLES)
            pe.wait_ge(c_rt, ROUTE * NG)

            def body3(i, on):
                if on(3):
                    e = pe.value_load(ti[0:1, 1, bass.ds(i - 3, 1)], min_val=0, max_val=E - 1)
                if on(1):
                    need(pe, e_n, i)
                    need(pe, e_xt, i - 2)
                    nc.tensor.transpose(bank[on.k(1)][:, 0:P], ex[:, on.k(1), :], ident).then_inc(e_tr, 1)
                if on(2):
                    need(pe, e_xt, i - 1)
                    need(pe, e_w1, i - 1)
                    need(pe, e_ht, i - 3)
                    for c in range(HC):
                        ins = mm(bank[2 + on.k(2)][:, c * P:(c + 1) * P], w1c[:, on.k(2), c * P:(c + 1) * P],
                                 ext[:, on.k(2), :], start=True, stop=True, skip_group_check=True)
                    ins.then_inc(e_f1, 1)
                if on(3):
                    need(pe, e_ht, i - 2)
                    need(pe, e_o, i - 4)
                    for c in range(HC):
                        ins = mm(bank[6 + on.k(3)][:, 0:D], hidt[:, on.k(3), c, :], w2_sb[:, bass.ds(e, 1), c, :],
                                 start=(c == 0), stop=(c == HC - 1))
                    ins.then_inc(e_f2, 1)
            tiles3(pe, body3, 3)

        @block.vector
        def _(dve):
            v_ = nc.vector

            def after(sem_, value):
                need(dve, sem_, value)
                if not isinstance(value, int):
                    dve.nop(nofuse=True)

            def step(ins, n):
                ins.then_inc(s_set, 1)
                dve.wait_ge(s_set, n)

            def set_up_weights():
                dve.wait_ge(s_cst, 32)
                dve.wait_ge(s_wtok, 16 * 3)
                step(v_.tensor_scalar(beta_bc[:, :], cst[:, C_ONE:C_ONE + P], cols[:, 1:2], None, ALU.mult), 1)
                step(v_.tensor_scalar(w_sc[:, :, :], w_raw[:, :, :], cols[:, 0:1], None, ALU.mult), 2)
                step(v_.memset(bias3[:, :, :], 0.0), 3)

            def set_up_biases():
                dve.wait_ge(s_bias_ps, 1)
                step(v_.tensor_copy(bias_f[:, 0, :], bank[0][:, 0:D]), 4)
                step(v_.tensor_copy(bias_f[:, 1, :], bank[1][:, 0:D]), 5)
                step(v_.tensor_copy(bias_hi[:, :, :], bias_f[:, :, :]), 6)
                step(v_.tensor_tensor(bias_r[:, :, :], bias_f[:, :, :], bias_hi[:, :, :], ALU.subtract), 7)
                step(v_.tensor_copy(bias_mid[:, :, :], bias_r[:, :, :]), 8)
                step(v_.tensor_tensor(bias_lo[:, :, :], bias_r[:, :, :], bias_mid[:, :, :], ALU.subtract), 9)
                step(v_.tensor_copy(bias3[0:32, :, :], bias_hi[0:32, :, :]), 10)
                step(v_.tensor_copy(bias3[32:64, :, :], bias_mid[32:64, :, :]), 11)
                step(v_.tensor_copy(bias3[64:96, :, :], bias_lo[64:96, :, :]), 12)

            def body1(u, par, runs):
                if isinstance(u, int) and u == NG:
                    token_stats(0)
                    token_means(0, 0)
                for t in range(T):
                    if runs(0):
                        slot = par * T + t
                        if isinstance(u, int):
                            dve.wait_ge(x_in[slot], 16 * (u // 4 + 1))
                        else:
                            dve.wait_ge(x_in[slot], (u - par) * 4 + 16)
                        if t == 0:
                            need(dve, a_coef, u - 1)
                        for j in range(TOK):
                            ins = v_.bn_stats(st1[:, par % 2, t * TOK + j, :], xs[:, slot, j, :])
                        if t == T - 1:
                            ins.then_inc(a_stats, 1)
                    if runs(2):
                        g, k = u - 2, (par - 2) % 2
                        if t == 0:
                            need(dve, a_coef, g + 1)
                        for j in (0, 1):
                            x_j, c = xs[:, (par - 2) % 4 * T + t, j, :], t * TOK + j
                            ins = v_.tensor_scalar(x_j, x_j, rs1[:, k, c:c + 1], nm1[:, k, c:c + 1], ALU.mult, ALU.add)
                        ins.then_inc(a_nv, 1)
                if isinstance(u, int) and u == 0:
                    set_up_weights()
                if isinstance(u, int) and u == 1:
                    set_up_biases()

            def token_stats(g):
                need(dve, a_out, g + 1)
                need(dve, b_stats, g)
                for i in range(T):
                    ins = v_.bn_stats(st2[:, i, :], tile(g * T + i))
                ins.then_inc(b_st, 1)

            def token_means(g, k):
                after(b_coef, g - 1)
                after(b_st, g + 1)
                for i in range(T):
                    ins = v_.bn_aggr(mv2[:, k, i, :], st2[:, i, :])
                ins.then_inc(b_stats, 1)
            groups(dve, body1, 2, 4, 4)

            dve.wait_ge(s_watt, 16)

            iota = cst[:, C_IOTA:C_IOTA + T * E].rearrange("p (t e) -> p t e", t=T)
            gate_ps = bank[1][:, PV_END:PV_END + T * E].rearrange("p (t e) -> p t e", t=T)
            pre_ps = bank[0][:, PV_END:PV_END + T * E].rearrange("p (t e) -> p t e", t=T)
            all_ps = bank[0][:, PV_END + T * E:PV_END + (T + 1) * E]

            def route(g, kr, n):
                bc = lambda a: a.unsqueeze(2).to_broadcast([P, T, E])
                need(dve, c_rt, ROUTE * g + n - 1)
                if n == 1:
                    need(dve, c_gate, g + 1)
                    ins = v_.tensor_reduce(r4[:, 0, :], gate_ps, X, ALU.max)
                if n == 2:
                    ins = v_.tensor_tensor(rt[:, 0], gate_ps, bc(r4[:, 0, :]), ALU.subtract)
                if n == 3:
                    ins = v_.scalar_tensor_tensor(rt[:, 2], rt[:, 0], 0.0, iota, ALU.is_equal, ALU.mult)
                if n == 4:
                    ins = v_.tensor_reduce(r4[:, 1, :], rt[:, 2], X, ALU.min)
                if n == 5:
                    ins = v_.tensor_tensor(oh_bf[:, :, :], iota, bc(r4[:, 1, :]), ALU.is_equal)
                if n == 6:
                    need(dve, c_exp, g + 1)
                    ins = v_.tensor_reduce(r4[:, 2, :], rt[:, 1], X, ALU.add)
                if n == 7:
                    ins = v_.scalar_tensor_tensor(rt[:, 3], oh_bf[:, :, :], 1.0, rt[:, 1], ALU.subtract, ALU.mult)
                if n == 8:
                    ins = v_.tensor_reduce(r4[:, 3, :], rt[:, 3], X, ALU.min)
                if n == 9:
                    ins = v_.scalar_tensor_tensor(r4[:, 4, :], r4[:, 2, :], 1e-9, r4[:, 3, :], ALU.mult, ALU.subtract)
                if n == 10:
                    need(dve, c_pre, g + 1)
                    ins = v_.tensor_tensor(rt[:, 4], pre_ps, base[:, :].unsqueeze(1).to_broadcast([P, T, E]), ALU.add)
                if n == 11:
                    ins = v_.tensor_tensor(base[:, :], all_ps, base[:, :], ALU.add)
                if n == 12:
                    ins = v_.tensor_tensor(rt[:, 5], rt[:, 4], oh_bf[:, :, :], ALU.mult)
                if n == 13:
                    ins = v_.tensor_reduce(r4[:, 5, :], rt[:, 5], X, ALU.add)
                if n == 14:
                    ins = v_.tensor_copy(pos[:, kr, :], r4[:, 5, :])
                if n == 15:
                    ins = v_.tensor_scalar(r4[:, 6, :], r4[:, 4, :], 1.0, None, ALU.add)
                if n == 16:
                    ins = v_.reciprocal(row[:, kr, :, GATE], r4[:, 6, :])
                ins.then_inc(c_rt, 1)

            def sent(g, kr):
                return g // 4 * 16 * T if isinstance(g, int) else (g - kr) * (4 * T)

            def body2(u, par, runs):
                k1 = (par - S1) % 2
                g1 = u - S1
                g4, kr = u - S4, (par - S4) % 4

                def mix(h, last):
                    ins = v_.tensor_scalar(kmix[:, k1, h, :], kt[:, k1, :], mix_sb[:, h:h + 1], None, ALU.mult)
                    if last:
                        ins.then_inc(b_kmv, 1)

                def routed(*steps):
                    if runs(S6):
                        for n in steps:
                            route(u - S6, (par - S6) % 4, n)

                for t in range(T):
                    if runs(S2):
                        n = (u - S2) * T + t
                        need(dve, b_sc, n + 1)
                        sc = bank[4 + t % 2][:, :].rearrange("p (h s) -> p h s", h=H)
                        v_.tensor_reduce(mx[:, t % 2, :], sc, X, ALU.max).then_inc(b_mx, 1)
                    routed((3, 6, 8, 14)[t])
                    if runs(S2):
                        dve.wait_ge(b_mx, n + 1)
                        need(dve, b_exp, n - 1)
                        v_.tensor_tensor(pr[:, t % 2, :, :], sc, mx[:, t % 2, :].unsqueeze(2).to_broadcast([P, H, SEQ]),
                                         ALU.subtract).then_inc(b_sub, 1)
                    if t == 0:
                        routed(4)
                        if runs(0):
                            token_stats(u)
                        routed(5)
                        if runs(0):
                            token_means(u, par % 2)
                    if t == 1 and runs(S1):
                        need(dve, b_kt, g1 + 1)
                        mix(0, last=False)
                    if t == 1 and runs(S4):
                        need(dve, c_wd, g4 + 1)
                        need(dve, b_bd, g4 + 1)
                        need(dve, c_scat[kr], sent(g4, kr))
                        v_.tensor_tensor(row[:, kr, :, 0:D], bank[3][:, :].rearrange("p (t d) -> p t d", t=T),
                                         tok_out[:, bass.ds(g4 * T, T), :], ALU.add).then_inc(c_res, 1)
                    if t in (1, 2) and runs(S1):
                        for h in ((1, 2, 3), (4, 5))[t - 1]:
                            mix(h, last=h == 5)
                    if t == 1 and runs(S1):
                        need(dve, b_v, 2 * g1 + 1)
                        need(dve, b_pv, T * (g1 - 1))
                        need(dve, b_cbs, 4 * g1)
                        src = bank[2][:, 0:T * VB].rearrange("p (b w) -> p b w", b=T)
                        v = src[:, :, 0:D // 2].rearrange("p b (h d) -> p b h d", h=HP)
                        v_.tensor_copy(cbf[:, :, 2:4, :].rearrange("p q t h -> p t q h"),
                                       src[0:SEQ, :, D // 2:VB].rearrange("p (t q) h -> p t q h", q=2))
                        v_.tensor_copy(vb[0:64, k1, T:2 * T, :, 0:DH], v[0:64])
                        v_.tensor_copy(vb[64:128, k1, T:2 * T, :, VW:VW + DH], v[64:128]).then_inc(b_vv, 1)
                    if t == 3:
                        routed(15)
                    s, tt = (S2, t - 2) if t > 1 else (S3, t + 2)
                    cp = bank[tt % 2][:, 0:PV_END].rearrange("p (a b c) -> p a b c", a=HP, b=2)
                    g, k = u - s, (par - s) % 2
                    n = g * T + tt
                    if runs(s):
                        need(dve, b_pv, n + 1)
                    if t == 2:
                        routed(9, 10)
                    if t == 3:
                        routed(16)
                        if runs(S5):
                            route(u - S5, (par - S5) % 4, 1)
                    if runs(s):
                        v_.reciprocal(rden[:, tt % 2, :, :], cp[:, :, :, DH]).then_inc(b_rd, 1)
                    if t == 1:
                        routed(7)
                    elif t == 2:
                        routed(11)
                    elif t == 3 and runs(S5):
                        route(u - S5, (par - S5) % 4, 2)
                    if runs(s):
                        dve.wait_ge(b_rd, n + 1)
                        if tt == 0:
                            need(dve, c_tr, g - 1)
                        v_.tensor_tensor(ctxn[:, k, tt, :].rearrange("p (a b c) -> p a b c", a=HP, b=2), cp[:, :, :, 0:DH],
                                         rden[:, tt % 2, :, :].unsqueeze(3).to_broadcast([P, HP, 2, DH]),
                                         ALU.mult).then_inc(b_cn, 1)
                    if t == 2:
                        routed(12)
                    if t == 2 and runs(S4):
                        dve.wait_ge(c_res, g4 + 1)
                        need(dve, c_stats, g4)
                        for i in range(T):
                            ins = v_.bn_stats(st3[:, i, :], row[:, kr, i, 0:D])
                        ins.then_inc(c_st, 1)
                    if t == 2:
                        routed(13)
                    if t == 2 and runs(S4):
                        after(c_small, SMALL3 * (g4 - 2) + 3)
                        after(c_st, g4 + 1)
                        for i in range(T):
                            ins = v_.bn_aggr(mv3[:, (par - S4) % 2, i, :], st3[:, i, :])
                        ins.then_inc(c_stats, 1)
            dve.wait_ge(s_const, 7)
            dve.wait_ge(s_vb, 4)
            groups(dve, body2, S6, 8, 4, start=1)

            dve.wait_ge(s_wexp, 32 * E)

            def tab(ins, n):
                ins.then_inc(s_tab, 1)
                dve.wait_ge(s_tab, n)
            cb_ = cst[0:1, C_BASE:C_BASE + E]
            tab(v_.tensor_copy(tei[:, 0, :], base[0:1, :]), 1)
            tab(v_.scalar_tensor_tensor(te[:, 0, :], base[0:1, :], float(P - 1), cb_, ALU.add, ALU.subtract), 2)
            tab(v_.tensor_copy(tei[:, 1, :], te[:, 0, :]), 3)
            tab(v_.tensor_scalar(tei[:, 1, :], tei[:, 1, :], 7, None, ALU.arith_shift_right), 4)
            tab(v_.tensor_copy(te[:, 1, :], tei[:, 1, :]), 5)
            tab(v_.tensor_copy(te[:, 2, :], te[:, 1, :]), 6)
            for e in range(1, E):
                tab(v_.tensor_tensor(te[:, 2, e:e + 1], te[:, 2, e - 1:e], te[:, 1, e:e + 1], ALU.add), 6 + e)
            tiles_i = cst[0:1, C_TILE:C_END].rearrange("p (i e) -> p i e", e=E)
            tab(v_.tensor_tensor(tg[:, 0], tiles_i, te[:, 2, :].unsqueeze(1).to_broadcast([1, NX, E]), ALU.is_ge), 12)
            tab(v_.tensor_tensor(tg[:, 1], tg[:, 0], te[:, 1, :].unsqueeze(1).to_broadcast([1, NX, E]), ALU.mult), 13)
            tab(v_.tensor_reduce(tn[:, 0, :], tg[:, 0], X, ALU.add), 14)
            tab(v_.tensor_reduce(tn[:, 1, :], tg[:, 1], X, ALU.add), 15)
            tab(v_.tensor_tensor(tn[:, 2, :], tiles_i[:, :, 0], tn[:, 1, :], ALU.subtract), 16)
            tab(v_.tensor_scalar(tn[:, 2, :], tn[:, 2, :], float(P), None, ALU.mult), 17)
            tab(v_.scalar_tensor_tensor(tn[:, 3, :], tn[:, 0, :], float(REGION), tn[:, 2, :], ALU.mult, ALU.add), 18)
            tab(v_.tensor_copy(ti[:, 0, :], tn[:, 3, :]), 19)
            tab(v_.tensor_scalar(ti[:, 1, :], tn[:, 0, :], float(E - 1), None, ALU.min), 20)

            def body3(i, on):
                if on(0):
                    dve.wait_ge(e_in[on.k(0, 8)], 16 * (i // 8 + 1) if isinstance(i, int) else (i - on.c) * 2 + 16)
                    need(dve, e_tr, i - 1)
                    r = er[:, on.k(0, 8), :]
                    v_.tensor_scalar(ex[:, on.k(0), :], r[:, 0:D], r[:, SCALE:SCALE + 1], r[:, SHIFT:SHIFT + 1],
                                     ALU.mult, ALU.add).then_inc(e_n, 1)
                    e = dve.value_load(ti[0:1, 1, bass.ds(i, 1)], min_val=0, max_val=E - 1)
                    need(dve, e_f1, i - 1)
                    v_.tensor_scalar(w1c[:, on.k(0), :], w1_sb[:, bass.ds(e, 1), :].rearrange("p o h -> p (o h)"),
                                     cols[:, 2:3], None, ALU.mult).then_inc(e_w1, 1)
                if on(4):
                    need(dve, e_f2, i - 3)
                    if not (isinstance(i, int) and i < 8):
                        need(dve, e_out[on.k(4, 4)], stored(i - 8, on.k(4, 4)))
                    r = er[:, on.k(4, 8), :]
                    v_.scalar_tensor_tensor(eo[:, on.k(4, 4), :], bank[6 + on.k(4)][:, 0:D], r[:, GATE:GATE + 1],
                                            r[:, 0:D], ALU.mult, ALU.add).then_inc(e_o, 1)
            tiles3(dve, body3, 4)


_OUT = (P, SEQ, D)


def kernel(x, L0_tok_ln_gamma, L0_tok_ln_beta, L0_tok_W, L0_tok_b, L0_attn_Wq, L0_attn_Wk, L0_attn_Wv, L0_attn_Wb,
           L0_attn_mixing, L0_attn_Wd, L0_attn_bd, L0_ffn_w_gating, L0_ffn_gamma, L0_ffn_w1, L0_ffn_w2):
    import concourse.bacc as bacc
    from concourse.bass_utils import run_bass_kernel_spmd

    c, i = constants()
    wv = np.reshape(np.transpose(L0_attn_Wv), (D, HP, 2, DH))
    arrays = {
        "x": x, "w_tok": L0_tok_W,
        "narrow": np.concatenate([np.reshape(L0_tok_ln_gamma, (D, 1)), np.reshape(L0_tok_ln_beta, (D, 1)),
                                  np.reshape(L0_ffn_gamma, (D, 1)),
                                  np.transpose(L0_attn_mixing), L0_ffn_w_gating], axis=1),
        "biases": np.concatenate([np.reshape(L0_tok_b, (1, D)), np.reshape(L0_attn_bd, (1, D))], axis=1),
        "w_att": np.concatenate([np.transpose(L0_attn_Wq), np.transpose(L0_attn_Wk), np.transpose(L0_attn_Wd),
                                 np.reshape(wv[:, :, 0], (D, D // 2)), np.transpose(L0_attn_Wb),
                                 np.reshape(wv[:, :, 1], (D, D // 2))], axis=1),
        "w1": L0_ffn_w1, "w2": L0_ffn_w2, "cf": c, "ci": i,
    }
    arrays = {f"in_{n}": np.ascontiguousarray(a) for n, a in arrays.items()}
    nc = bacc.Bacc("TRN2", target_bir_lowering=False, num_devices=1)
    args = [nc.dram_tensor(n, a.shape, mybir.dt.from_np(a.dtype), kind="ExternalInput").ap() for n, a in arrays.items()]
    rows = nc.dram_tensor("rows", ((E * REGION + SPARE * P), ROWW), F32).ap()
    out = nc.dram_tensor("out", (N, D), F32, kind="ExternalOutput").ap()
    build(nc, *args, rows, out)
    r = run_bass_kernel_spmd(nc, [arrays], core_ids=[0])
    return np.reshape(r.results[0]["out"], _OUT)
```
